# Optimizing a Trainium2 kernel written in Bass

```python
import numpy as np
import jax
import jax.numpy as jnp

def _softmax(x, axis=-1):
    return jax.nn.softmax(x, axis=axis)

def _gelu(x):
    return jax.nn.gelu(x, approximate=True)

def _silu(x):
    return jax.nn.silu(x)

def _sigmoid(x):
    return jax.nn.sigmoid(x)

def _layernorm(x, axis=-1, eps=1e-05):
    m = jnp.mean(x, axis=axis, keepdims=True)
    v = jnp.var(x, axis=axis, keepdims=True)
    return (x - m) / jnp.sqrt(v + eps)

def _scatter_add(tgt, idx, src, axis=0):
    return tgt.at[idx].add(src)

def _segment_sum(src, seg, n):
    return jax.ops.segment_sum(src, seg, n)
kernel_name = 'mk_adj_preln_d2_adj_r2_6ecf9d'

def setup_inputs(seed: int=0):
    np.random.seed(seed)
    _w = jnp.asarray

    def _rec_inputs():
        import jax
        import jax.numpy as jnp
        _gk = jax.random.key(seed)
        x = -0.0005207 + 1.001 * jax.random.normal(jax.random.fold_in(_gk, 1), (1354, 256), jnp.float32)
        _w = (1.0 + jnp.arange(1354, dtype=jnp.float32)) ** (-0.5)
        _w = _w / _w.mean()
        _pij = jnp.clip(0.0014771 * _w[:, None] * _w[None, :], 0.0, 1.0)
        _a = jax.random.uniform(jax.random.fold_in(_gk, 2), (1354, 1354)) < _pij
        _a = jnp.logical_or(_a, jnp.eye(1354, dtype=bool))
        _af = _a.astype(jnp.float32)
        _af = _af * jax.random.uniform(jax.random.fold_in(_gk, 3), (1354, 1354), jnp.float32, 0.05, 1)
        adj = _af
        return (x, adj)
    x, adj = _rec_inputs()

    def _L0_gnn_setup():
        import jax, jax.numpy as jnp
        import numpy as np
        N, D_IN, D_ATTN, STEPS, P_NUC, TAU = (2048, 256, 64, 2, 0.9, 1.0)
        LN_EPS = 1e-05

        def _xavier(key, shape):
            fan_in, fan_out = (shape[-2], shape[-1])
            lim = np.sqrt(6.0 / (fan_in + fan_out))
            return jax.random.uniform(key, shape, jnp.float32, -lim, lim)

        def _adj_from_feats(Xa, W1, W2, W3):
            Q = Xa @ W1
            K = Xa @ W3
            logits = Q @ W2 @ K.T / TAU
            idx = jnp.argsort(-logits, axis=1)
            vals = jnp.take_along_axis(logits, idx, axis=1)
            csum = jnp.cumsum(jax.nn.softmax(vals, axis=1), axis=1)
            k_i = jnp.sum(csum < P_NUC, axis=1) + 1
            ranks = jnp.arange(logits.shape[1])[None, :]
            keep_sorted = ranks < k_i[:, None]
            inv = jnp.argsort(idx, axis=1)
            keep = jnp.take_along_axis(keep_sorted, inv, axis=1)
            masked = jnp.where(keep, logits, -jnp.inf)
            return jax.nn.softmax(masked, axis=1)
        key = jax.random.key(seed)
        ks = jax.random.split(key, 9)
        return {'X': jax.random.normal(ks[0], (N, D_IN), jnp.float32), 'S': jax.random.uniform(ks[1], (N, N), jnp.float32), 'W1': _xavier(ks[2], (D_IN, D_ATTN)), 'W2': _xavier(ks[3], (D_ATTN, D_ATTN)), 'W3': _xavier(ks[4], (D_IN, D_ATTN)), 'U1': _xavier(ks[5], (STEPS, D_IN, D_IN)), 'U2': _xavier(ks[6], (STEPS, D_IN, D_IN)), 'U3': _xavier(ks[7], (STEPS, D_IN, D_IN)), 'gamma': jnp.ones((D_IN,), jnp.float32), 'beta': jnp.zeros((D_IN,), jnp.float32)}
    _L0_gnn_all = _L0_gnn_setup()
    _L0_gnn_in = {k: v for k, v in _L0_gnn_all.items() if k in ('W1', 'W2', 'W3', 'U1', 'U2', 'U3', 'gamma', 'beta')}
    del _L0_gnn_all

    def _L1_gnn_setup():
        import jax, jax.numpy as jnp
        import numpy as np
        N = 4096
        D_IN = 256
        D_OUT = 256
        NEG_BIG = -9000000000000000.0
        key = jax.random.key(seed)
        kx, ka, kw, kb, kn, ke = jax.random.split(key, 6)
        x = jax.random.normal(kx, (N, D_IN), dtype=jnp.float32)
        adj = (jax.random.uniform(ka, (N, N)) > 0.9).astype(jnp.float32)
        stdv = 1.0 / np.sqrt(D_OUT)
        weight = jax.random.uniform(kw, (D_IN, D_OUT), minval=-stdv, maxval=stdv, dtype=jnp.float32)
        bias = jax.random.uniform(kb, (D_OUT,), minval=-stdv, maxval=stdv, dtype=jnp.float32)
        node_w = jax.random.uniform(kn, (D_IN, 1), minval=-1.0, maxval=1.0, dtype=jnp.float32)
        stdv_e = 1.0 / np.sqrt(D_IN)
        edge_w = jax.random.uniform(ke, (D_IN, D_IN), minval=-stdv_e, maxval=stdv_e, dtype=jnp.float32)
        return {'x': x, 'adj': adj, 'weight': weight, 'bias': bias, 'node_w': node_w, 'edge_w': edge_w}
    _L1_gnn_all = _L1_gnn_setup()
    _L1_gnn_in = {k: v for k, v in _L1_gnn_all.items() if k in ('weight', 'bias', 'node_w', 'edge_w')}
    del _L1_gnn_all
    return {'x': x, 'adj': adj, 'L0_gnn_W1': _L0_gnn_in['W1'], 'L0_gnn_W2': _L0_gnn_in['W2'], 'L0_gnn_W3': _L0_gnn_in['W3'], 'L0_gnn_U1': _L0_gnn_in['U1'], 'L0_gnn_U2': _L0_gnn_in['U2'], 'L0_gnn_U3': _L0_gnn_in['U3'], 'L0_gnn_gamma': _L0_gnn_in['gamma'], 'L0_gnn_beta': _L0_gnn_in['beta'], 'L1_gnn_weight': _L1_gnn_in['weight'], 'L1_gnn_bias': _L1_gnn_in['bias'], 'L1_gnn_node_w': _L1_gnn_in['node_w'], 'L1_gnn_edge_w': _L1_gnn_in['edge_w']}

def reference(x, adj, L0_gnn_W1, L0_gnn_W2, L0_gnn_W3, L0_gnn_U1, L0_gnn_U2, L0_gnn_U3, L0_gnn_gamma, L0_gnn_beta, L1_gnn_weight, L1_gnn_bias, L1_gnn_node_w, L1_gnn_edge_w):
    import jax
    import jax.numpy as jnp

    def _L0_gnn_ref(X, S, W1, W2, W3, U1, U2, U3, gamma, beta):
        import jax, jax.numpy as jnp
        import numpy as np
        N, D_IN, D_ATTN, STEPS, P_NUC, TAU = (2048, 256, 64, 2, 0.9, 1.0)
        LN_EPS = 1e-05

        def _xavier(key, shape):
            fan_in, fan_out = (shape[-2], shape[-1])
            lim = np.sqrt(6.0 / (fan_in + fan_out))
            return jax.random.uniform(key, shape, jnp.float32, -lim, lim)

        def _adj_from_feats(Xa, W1, W2, W3):
            Q = Xa @ W1
            K = Xa @ W3
            logits = Q @ W2 @ K.T / TAU
            idx = jnp.argsort(-logits, axis=1)
            vals = jnp.take_along_axis(logits, idx, axis=1)
            csum = jnp.cumsum(jax.nn.softmax(vals, axis=1), axis=1)
            k_i = jnp.sum(csum < P_NUC, axis=1) + 1
            ranks = jnp.arange(logits.shape[1])[None, :]
            keep_sorted = ranks < k_i[:, None]
            inv = jnp.argsort(idx, axis=1)
            keep = jnp.take_along_axis(keep_sorted, inv, axis=1)
            masked = jnp.where(keep, logits, -jnp.inf)
            return jax.nn.softmax(masked, axis=1)
        n = X.shape[0]
        S = S + jnp.eye(n, dtype=X.dtype)
        Rf = S / jnp.clip(S.sum(axis=1, keepdims=True), 1e-12)
        Rb = S / jnp.clip(S.sum(axis=0), 1e-12)[:, None]
        Xf, Xb, Xa = (X, X, X)
        Z = jnp.zeros_like(X)
        for s in range(STEPS):
            A = _adj_from_feats(Xa, W1, W2, W3)
            Xf = Rf @ Xf
            Xb = Rb @ Xb
            Xa = A @ Xa
            Z = Z + (Xf @ U1[s] + Xb @ U2[s] + Xa @ U3[s])
        Y = X + Z
        mu = Y.mean(axis=-1, keepdims=True)
        var = Y.var(axis=-1, keepdims=True)
        return (Y - mu) / jnp.sqrt(var + LN_EPS) * gamma + beta

    def _L1_gnn_ref(x, adj, weight, bias, node_w, edge_w):
        import jax, jax.numpy as jnp
        import numpy as np
        N = 4096
        D_IN = 256
        D_OUT = 256
        NEG_BIG = -9000000000000000.0
        node_att = jax.nn.softmax(x @ node_w, axis=0)
        h = x @ edge_w
        e = h @ h.T
        e = jnp.where(adj > 0, e, NEG_BIG)
        edge_att = jax.nn.softmax(e, axis=1)
        combined_att = node_att * edge_att
        support = x @ weight
        output = adj * combined_att @ support
        return output + bias
    h = jnp.maximum(_layernorm(x, axis=-1), 0.0)
    x = x + _L0_gnn_ref(h, adj, L0_gnn_W1, L0_gnn_W2, L0_gnn_W3, L0_gnn_U1, L0_gnn_U2, L0_gnn_U3, L0_gnn_gamma, L0_gnn_beta)
    h = jnp.maximum(_layernorm(x, axis=-1), 0.0)
    x = x + _L1_gnn_ref(h, adj, L1_gnn_weight, L1_gnn_bias, L1_gnn_node_w, L1_gnn_edge_w)
    return x

_drawn_inputs = setup_inputs


def setup_inputs(seed=0):
    import zlib

    import numpy as np

    out = dict(_drawn_inputs(seed))
    spreads = {'L0_gnn_gamma': (1.0, 0.2), 'L0_gnn_beta': (0.0, 0.1)}
    factors = {'L1_gnn_weight': 8.0, 'L1_gnn_bias': 2.719, 'L1_gnn_node_w': 8.0}
    for name, (base, spread) in spreads.items():
        noise = np.random.default_rng([zlib.crc32(name.encode()), seed]).standard_normal(out[name].shape)
        drawn = base * np.exp(spread * noise) if base else spread * noise
        out[name] = jnp.asarray(drawn.astype(out[name].dtype))
    for name, factor in factors.items():
        out[name] = (out[name] * factor).astype(out[name].dtype)
    return out
```

```python
from contextlib import ExitStack

import numpy as np

import concourse.bass as bass
from concourse import mybir

F32 = mybir.dt.float32
I32 = mybir.dt.int32
ALU = mybir.AluOpType
ACT = mybir.ActivationFunctionType
AX = mybir.AxisListType

P = 128
P_NUC = 0.9
LN_EPS = 1e-5
NEG_BIG = -9.0e15
HUGE = 1.0e30
HALVINGS = 7


def gnn_block(nc, x, adj, adj_t, W1, W2, W3, U1, U2, U3, gamma, beta, weight, bias, node_w, edge_w, out):
    N, D = x.shape
    H = W1.shape[1]
    NT = -(-N // P)
    FULL = N // P
    TAIL = N - FULL * P
    DC = D // P
    BANK = 512
    NB = -(-N // BANK)
    TB = BANK // P
    PAD = 8
    assert DC == 2 and NT == FULL + 1 and TAIL > 0 and NB == 3 and H <= P

    def rows(t):
        return P if t < FULL else TAIL

    def nodes(t):
        return slice(t * P, t * P + rows(t))

    def chunk(b):
        return slice(b * BANK, min(N, (b + 1) * BANK))

    LOWEST = (1.0 - P_NUC) / N * 0.999
    SPAN = float(np.log(1.0 / LOWEST))
    MAX_ROUNDS = float(-(-N // 8))

    with ExitStack() as ctx:
        def sb(name, shape, dt=F32):
            return ctx.enter_context(nc.sbuf_tensor(name, shape, dt))

        def sem(name):
            return ctx.enter_context(nc.semaphore(name))

        reg_adj = sb("reg_adj", [P, NT, N])
        reg_rows = sb("reg_rows", [P, NT, N])
        reg_h = sb("reg_h", [P, NT, D + 1])
        reg_mix = sb("reg_mix", [P, NT * 2 * D])
        reg_z = sb("reg_z", [P, NT * D])
        reg_at = sb("reg_at", [P, 2, NT * P])
        below = sb("below", [P, N + PAD])

        ST = reg_adj
        E = reg_rows
        h = reg_h[:, :, 0:D]
        hT = reg_z[:, 0:DC * N].rearrange("p (c n) -> p c n", c=DC)
        Z = reg_z[:, :].rearrange("p (t d) -> p t d", t=NT)
        FB = reg_mix[:, :].rearrange("p (t d) -> p t d", t=NT)
        Xa = reg_mix[:, 0:NT * D].rearrange("p (t d) -> p t d", t=NT)
        XaT = reg_mix[:, NT * D:NT * D + DC * N].rearrange("p (c n) -> p c n", c=DC)
        h2T = reg_mix[:, 0:DC * N].rearrange("p (c n) -> p c n", c=DC)
        hhT = reg_mix[:, NT * D:NT * D + DC * N].rearrange("p (c n) -> p c n", c=DC)
        AT = reg_at[:, :, :].rearrange("p b (j r) -> p b j r", j=NT)
        Q2T = reg_at[0:H, 0, 0:N]
        KT = reg_at[0:H, 1, 0:N]
        QT = below[0:H, 0:N]
        spare = reg_rows[:, 0:5, :].rearrange("p t n -> p (t n)")
        xres = spare[:, 0:NT * D].rearrange("p (t d) -> p t d", t=NT)
        o = NT * D
        gam, bet, bia = (spare[:, o + i * D:o + (i + 1) * D] for i in range(3))
        o += 3 * D
        EW = spare[:, o:o + DC * D].rearrange("p (c d) -> p c d", c=DC)
        o += DC * D
        WN = spare[:, o:o + DC * (D + 1)].rearrange("p (c d) -> p c d", c=DC)
        assert o + DC * (D + 1) <= 5 * N
        adj_n = reg_adj
        support = reg_h
        negm = reg_rows[:, 5:7, :]
        em = reg_rows[:, 7:9, :]

        W1s = sb("W1s", [P, DC, H])
        W3s = sb("W3s", [P, DC, H])
        W2s = sb("W2s", [H, H])
        U12 = sb("U12", [P, 2, 2, DC, D])
        U3s = sb("U3s", [P, 2, DC, D])
        turned = sb("turned", [P, 2, BANK])
        FB2 = sb("FB2", [P, 2, BANK])
        ident = sb("ident", [P, P])
        ones_all = sb("ones_all", [P, P])
        ones = ones_all[:, 0:1]
        ones_row = ones_all[0:1, :]

        stats = sb("stats", [P, NT, 6])
        mv = sb("mv", [P, NT, 2])
        var = sb("var", [P, NT])
        sd = sb("sd", [P, NT])
        rstd = sb("rstd", [P, NT])
        t0 = sb("t0", [P, NT])
        t1 = sb("t1", [P, NT])
        nmr = sb("nmr", [P, NT])
        nmax = sb("nmax", [P, NT])
        tot = sb("tot", [P, NT])
        rest = sb("rest", [P, NT])
        goal = sb("goal", [P, NT])
        mid = sb("mid", [P, NT])
        mass = sb("mass", [P, NT])
        reached = sb("reached", [P, NT])
        lo = sb("lo", [P, NT])
        hi = sb("hi", [P, NT])
        mass_hi = sb("mass_hi", [P, NT])
        lo_c = sb("lo_c", [P, NT])
        hi_c = sb("hi_c", [P, NT])
        mass_c = sb("mass_c", [P, NT])
        factor = sb("factor", [P, HALVINGS + 1])
        need = sb("need", [P, NT])
        rounds_f = sb("rounds_f", [NT, 1])
        rounds_i = sb("rounds_i", [NT, 1], I32)
        top = sb("top", [P, 8])
        taken = sb("taken", [P, 8])
        zero8 = sb("zero8", [P, 8])
        cum = sb("cum", [P, 9])
        kept = sb("kept", [P, NT])
        rkept = sb("rkept", [P, NT])
        csum = sb("csum", [P, NT])
        inv_c = sb("inv_c", [P, NT])
        inv_r = sb("inv_r", [P, NT])
        rc = sb("rc", [P, NT])
        nm1 = sb("nm1", [P, NT])
        psum_row = sb("psum_row", [P, NT])
        score = sb("score", [P, NT])
        psum_max = sb("psum_max", [P, NT])
        nmx = sb("nmx", [P, 1])
        nall = sb("nall", [P, 1])
        natt = sb("natt", [P, NT])
        ncol = sb("ncol", [P, 1])
        ntot = sb("ntot", [P, 1])
        final = sb("final", [P, NT])

        ps = ctx.enter_context(nc.psum_tensor("ps", [P, 8, BANK], F32))

        x_in, w_in, u_in, st_in, sp_in, adj_in, out_done = (
            sem(n) for n in ("x_in", "w_in", "u_in", "st_in", "sp_in", "adj_in", "out_done"))
        st_diag = sem("st_diag")
        const_ready = sem("const_ready")
        var_ready, sd_ready, norm_ready = sem("var_ready"), sem("sd_ready"), sem("norm_ready")
        h_ready, h_turned, hT_ready = sem("h_ready"), sem("h_turned"), sem("hT_ready")
        qk_done, qk_copied = sem("qk_done"), sem("qk_copied")
        logits_done, max_ready, exp_done = sem("logits_done"), sem("max_ready"), sem("exp_done")
        rsum_done, csum_done, inv_ready = sem("rsum_done"), sem("csum_done"), sem("inv_ready")
        sx_done, fb_ready, fb_turned, fbT_ready = sem("sx_done"), sem("fb_ready"), sem("fb_turned"), sem("fbT_ready")
        z_done, z_ready = sem("z_done"), sem("z_ready")
        need_ready, need_turned = sem("need_ready"), sem("need_turned")
        A_ready, A_turned, AT_ready = sem("A_ready"), sem("A_turned"), sem("AT_ready")
        ax_done, xa_ready, xa_turned, xaT_ready = sem("ax_done"), sem("xa_ready"), sem("xa_turned"), sem("xaT_ready")
        y_done, y_ready = sem("y_done"), sem("y_ready")
        x1_ready, h2_ready = sem("x1_ready"), sem("h2_ready")
        h2_turned, h2T_ready, hh_done, hhT_ready = sem("h2_turned"), sem("h2T_ready"), sem("hh_done"), sem("hhT_ready")
        sup_done, sup_ready = sem("sup_done"), sem("sup_ready")
        negm_ready, e_done, em_ready, p_ready, pa_ready = (
            sem(n) for n in ("negm_ready", "e_done", "em_ready", "p_ready", "pa_ready"))
        pa_turned, paT_ready, out_sum, out_ready = (
            sem(n) for n in ("pa_turned", "paT_ready", "out_sum", "out_ready"))
        score_max, score_all, score_exp, score_sum, score_tot = (
            sem(n) for n in ("score_max", "score_all", "score_exp", "score_sum", "score_tot"))
        xb_ready = sem("xb_ready")

        block = ctx.enter_context(nc.Block())

        @block.sync
        def _(sp):
            sp.dma_start(E[:, 0:FULL, 0:D], x[0:FULL * P, :].rearrange("(t p) d -> p t d", p=P)).then_inc(x_in, 16)
            sp.dma_start(E[0:TAIL, FULL, 0:D], x[FULL * P:N, :]).then_inc(x_in, 16)
            sp.dma_start(W1s[:, :, :], W1.rearrange("(c p) n -> p c n", p=P)).then_inc(w_in, 16)
            sp.dma_start(W3s[:, :, :], W3.rearrange("(c p) n -> p c n", p=P)).then_inc(w_in, 16)
            sp.dma_start(W2s[:, :], W2).then_inc(w_in, 16)
            for k in range(NT):
                sp.dma_start(ST[0:rows(k), k, :], adj_t[nodes(k), :]).then_inc(st_in, 16)
            for s in range(2):
                for d, U in enumerate((U1, U2)):
                    sp.dma_start(U12[:, s, d, :, :], U[s, :, :].rearrange("(c p) n -> p c n", p=P)).then_inc(u_in, 16)
                sp.dma_start(U3s[:, s, :, :], U3[s, :, :].rearrange("(c p) n -> p c n", p=P)).then_inc(u_in, 16)
            sp.wait_ge(sx_done, 2 * NT)
            for t in range(NT):
                sp.dma_start(adj_n[0:rows(t), t, :], adj[nodes(t), :]).then_inc(adj_in, 16)
            sp.wait_ge(A_turned, NT + 5)
            sp.dma_start(xres[:, 0:FULL, :], x[0:FULL * P, :].rearrange("(t p) d -> p t d", p=P)).then_inc(sp_in, 16)
            sp.dma_start(xres[0:TAIL, FULL, :], x[FULL * P:N, :]).then_inc(sp_in, 16)
            for dst, src in ((gam, gamma), (bet, beta), (bia, bias)):
                sp.dma_start(dst, src.partition_broadcast(P)).then_inc(sp_in, 16)
            sp.dma_start(EW, edge_w.rearrange("(c p) n -> p c n", p=P)).then_inc(sp_in, 16)
            sp.dma_start(WN[:, :, 0:D], weight.rearrange("(c p) n -> p c n", p=P)).then_inc(sp_in, 16)
            with nc.allow_non_contiguous_dma(reason="node_w is one column of a few hundred values"):
                sp.dma_start(WN[:, :, D:D + 1], node_w.rearrange("(c p) n -> p c n", p=P)).then_inc(sp_in, 16)
            for t in range(NT):
                sp.wait_ge(out_ready, t + 1)
                sp.dma_start(out[nodes(t), :], Z[0:rows(t), t, :]).then_inc(out_done, 16)
            sp.wait_ge(out_done, 16 * NT)

        @block.gpsimd
        def _(pool):
            nc.gpsimd.memset(ident[:, :], 0.0).then_inc(const_ready, 1)
            nc.gpsimd.memset(ones_all[:, :], 1.0).then_inc(const_ready, 1)
            pool.wait_ge(const_ready, 2)
            nc.gpsimd.affine_select(out=ident[:, :], in_=ident[:, :], compare_op=ALU.not_equal, fill=1.0, base=0,
                                    pattern=[[-1, P]], channel_multiplier=1).then_inc(const_ready, 1)
            pool.wait_ge(const_ready, 3)
            for k in range(NT):
                r = rows(k)
                pool.wait_ge(st_in, 16 * NT)
                nc.gpsimd.tensor_tensor(ST[0:r, k, nodes(k)], ST[0:r, k, nodes(k)], ident[0:r, 0:r],
                                        ALU.add).then_inc(st_diag, 1)
            for t in range(NT):
                r = rows(t)
                pool.wait_ge(x1_ready, t + 1)
                pool.wait_ge(h2_ready, t + 1)
                nc.gpsimd.tensor_tensor(Z[0:r, t, :], Z[0:r, t, :], bia[0:r, :], ALU.add).then_inc(xb_ready, 1)
            for t in range(NT):
                r = rows(t)
                pool.wait_ge(adj_in, 16 * NT)
                pool.wait_ge(A_turned, 2 * NT)
                if t >= 2:
                    pool.wait_ge(em_ready, t - 1)
                nc.gpsimd.tensor_scalar(negm[0:r, t % 2, :], adj_n[0:r, t, :], 0.0, NEG_BIG,
                                        ALU.is_le, ALU.mult).then_inc(negm_ready, 1)

        @block.scalar
        def _(act):
            def roots(n):
                act.wait_ge(var_ready, n + 1)
                nc.scalar.activation(sd[:, :], var[:, :], ACT.Sqrt).then_inc(sd_ready, 1)

            def copy(dst, src):
                return nc.scalar.activation(dst, src, ACT.Copy)

            roots(0)
            act.wait_ge(norm_ready, 1)
            for t in range(NT):
                r = rows(t)
                nc.scalar.activation(h[0:r, t, :], E[0:r, t, 0:D], ACT.Relu, bias=nmr[0:r, t:t + 1],
                                     scale=rstd[0:r, t:t + 1]).then_inc(h_ready, 1)

            def projections(s):
                act.wait_ge(qk_done, 3 * s + 1)
                for b in range(NB):
                    n = N - BANK * b if b == NB - 1 else BANK
                    i = copy(QT[:, chunk(b)], ps[0:H, b, 0:n])
                i.then_inc(qk_copied, 1)
                act.wait_ge(qk_done, 3 * s + 3)
                for b in range(NB):
                    n = N - BANK * b if b == NB - 1 else BANK
                    i = copy(Q2T[:, chunk(b)], ps[0:H, b, 0:n])
                i.then_inc(qk_copied, 1)

            def exps(s):
                for t in range(NT):
                    r = rows(t)
                    act.wait_ge(max_ready, s * NT + t + 1)
                    nc.scalar.activation(E[0:r, t, :], logits_of(t)[0:r, :], ACT.Exp, bias=nmax[0:r, t:t + 1],
                                         accum_out=tot[0:r, t:t + 1]).then_inc(exp_done, 1)

            def turned_rows(s):
                for t in range(NT + 2):
                    if t < NT:
                        r, b = rows(t), t % 2
                        g = s * NT + t
                        act.wait_ge(A_turned, g + 1)
                        if g >= 2:
                            act.wait_ge(ax_done, g - 1)
                        if s == 1 and t < 2:
                            act.wait_ge(logits_done, 2 * NT)
                        for k in range(NB):
                            j0, j1 = k * TB, min(FULL, (k + 1) * TB)
                            src = ps[:, 3 * b + k, :].rearrange("p (j r) -> p j r", j=TB)[:, 0:j1 - j0, 0:r]
                            copy(AT[:, b, j0:j1, 0:r], src)
                        copy(AT[0:TAIL, b, FULL, 0:r],
                             ps[0:TAIL, 3 * b + NB - 1, (FULL % TB) * P:(FULL % TB) * P + r]).then_inc(AT_ready, 1)
                    if t >= 2:
                        u = t - 2
                        r, b = rows(u), u % 2
                        act.wait_ge(xa_turned, s * NT + u + 1)
                        if s == 0:
                            src = ps[:, 6 + b, D:2 * D].rearrange("p (c r) -> p c r", c=DC)[:, :, 0:r]
                            copy(XaT[:, :, nodes(u)], src).then_inc(xaT_ready, 1)
                        else:
                            if u >= 2:
                                act.wait_ge(y_done, u - 1)
                            copy(turned[:, b, 0:D], ps[:, 6 + b, D:2 * D]).then_inc(xaT_ready, 1)
                            act.wait_ge(y_done, u + 1)
                            copy(Z[0:r, u, :], ps[0:r, 6 + b, 0:D]).then_inc(y_ready, 1)

            def diffusion(s):
                for t in range(NT + 2):
                    if t < NT:
                        r, b = rows(t), t % 2
                        act.wait_ge(sx_done, s * NT + t + 1)
                        if s == 0:
                            nc.scalar.activation(FB[0:r, t, 0:D], ps[0:r, b, 0:D], ACT.Copy, scale=inv_r[0:r, t:t + 1])
                            nc.scalar.activation(FB[0:r, t, D:2 * D], ps[0:r, b, 0:D], ACT.Copy,
                                                 scale=inv_c[0:r, t:t + 1]).then_inc(fb_ready, 1)
                        else:
                            if t >= 2:
                                act.wait_ge(fb_turned, s * NT + t - 1)
                            nc.scalar.activation(FB2[0:r, b, 0:D], ps[0:r, b, 0:D], ACT.Copy, scale=inv_r[0:r, t:t + 1])
                            nc.scalar.activation(FB2[0:r, b, D:2 * D], ps[0:r, b, D:2 * D], ACT.Copy,
                                                 scale=inv_c[0:r, t:t + 1]).then_inc(fb_ready, 1)
                    if 1 <= t <= NT:
                        u = t - 1
                        b = u % 2
                        act.wait_ge(fb_turned, s * NT + u + 1)
                        if s * NT + u >= 2:
                            act.wait_ge(z_done, s * NT + u - 1)
                        copy(turned[:, b, :], ps[:, 2 + b, :]).then_inc(fbT_ready, 1)
                    if t >= 2:
                        u = t - 2
                        act.wait_ge(z_done, s * NT + u + 1)
                        copy(Z[0:rows(u), u, :], ps[0:rows(u), 4 + u % 2, 0:D]).then_inc(z_ready, 1)

            def logits_of(t):
                return ps[:, 3 * (t % 2):3 * (t % 2) + NB, :].rearrange("p b n -> p (b n)")[:, 0:N]

            projections(0)
            exps(0)
            act.wait_ge(st_diag, NT)
            for k in range(NT):
                r = rows(k)
                nc.scalar.activation(ST[0:r, k, :], ST[0:r, k, :], ACT.Copy, accum_out=csum[0:r, k:k + 1])
            nc.scalar.drain().then_inc(csum_done, 1)
            act.wait_ge(inv_ready, 1)
            diffusion(0)
            diffusion(1)
            turned_rows(0)
            projections(1)
            exps(1)
            turned_rows(1)

            roots(1)
            roots(2)
            act.wait_ge(norm_ready, 3)
            for t in range(NT):
                r = rows(t)
                nc.scalar.activation(h[0:r, t, :], Z[0:r, t, :], ACT.Relu, bias=nmr[0:r, t:t + 1],
                                     scale=rstd[0:r, t:t + 1]).then_inc(h2_ready, 1)
                if t >= 1:
                    u = t - 1
                    act.wait_ge(h2_turned, u + 1)
                    src = ps[:, 6 + u % 2, 0:D].rearrange("p (c r) -> p c r", c=DC)[:, :, 0:rows(u)]
                    copy(h2T[:, :, nodes(u)], src).then_inc(h2T_ready, 1)
            u = NT - 1
            act.wait_ge(h2_turned, u + 1)
            src = ps[:, 6 + u % 2, 0:D].rearrange("p (c r) -> p c r", c=DC)[:, :, 0:rows(u)]
            copy(h2T[:, :, nodes(u)], src).then_inc(h2T_ready, 1)
            for m in range(DC):
                act.wait_ge(hh_done, m + 1)
                for b in range(NB):
                    n = N - BANK * b if b == NB - 1 else BANK
                    i = copy(hhT[:, m, chunk(b)], ps[:, 3 * m + b, 0:n])
                i.then_inc(hhT_ready, 1)
            for t in range(NT):
                r = rows(t)
                act.wait_ge(sup_done, t + 1)
                copy(support[0:r, t, :], ps[0:r, 6 + t % 2, 0:D + 1]).then_inc(sup_ready, 1)
            act.wait_ge(score_all, 1)
            nc.scalar.activation(natt[:, 0:FULL], support[:, 0:FULL, D], ACT.Exp, bias=nall[:, :])
            nc.scalar.activation(natt[0:TAIL, FULL:NT], support[0:TAIL, FULL, D:D + 1], ACT.Exp,
                                 bias=nall[0:TAIL, :]).then_inc(score_exp, 1)
            for t in range(NT + 1):
                if t < NT:
                    r, b = rows(t), t % 2
                    act.wait_ge(em_ready, t + 1)
                    nc.scalar.activation(em[0:r, b, :], em[0:r, b, :], ACT.Exp, bias=nm1[0:r, t:t + 1],
                                         accum_out=psum_row[0:r, t:t + 1]).then_inc(p_ready, 1)
                if t >= 1:
                    u = t - 1
                    r, b = rows(u), u % 2
                    act.wait_ge(pa_turned, u + 1)
                    if u >= 2:
                        act.wait_ge(out_sum, u - 1)
                    for k in range(NB):
                        j0, j1 = k * TB, min(FULL, (k + 1) * TB)
                        src = ps[:, 3 * b + k, :].rearrange("p (j r) -> p j r", j=TB)[:, 0:j1 - j0, 0:r]
                        copy(AT[:, b, j0:j1, 0:r], src)
                    copy(AT[0:TAIL, b, FULL, 0:r],
                         ps[0:TAIL, 3 * b + NB - 1, (FULL % TB) * P:(FULL % TB) * P + r]).then_inc(paT_ready, 1)

        @block.vector
        def _(dve):
            V = nc.vector

            def fence():
                V.drain()

            def inverse_roots(n):
                V.tensor_scalar(var[:, :], mv[:, :, 1], LN_EPS, None, ALU.add)
                V.drain().then_inc(var_ready, 1)
                dve.wait_ge(sd_ready, n + 1)
                V.reciprocal(rstd[:, :], sd[:, :])
                fence()
                V.tensor_tensor(t0[:, :], rstd[:, :], rstd[:, :], ALU.mult)
                fence()
                V.tensor_tensor(t0[:, :], t0[:, :], var[:, :], ALU.mult)
                fence()
                V.tensor_scalar(t0[:, :], t0[:, :], -0.5, 1.5, ALU.mult, ALU.add)
                fence()
                V.tensor_tensor(rstd[:, :], rstd[:, :], t0[:, :], ALU.mult)
                fence()
                V.scalar_tensor_tensor(nmr[:, :], mv[:, :, 0], -1.0, rstd[:, :], ALU.mult, ALU.mult)
                V.drain().then_inc(norm_ready, 1)

            V.memset(mv[:, :, :], 1.0)
            V.memset(zero8[:, :], 0.0)
            V.memset(tot[:, :], 1.0)
            V.memset(mass[:, :], 0.0)
            V.memset(need[:, :], 0.0)
            V.memset(csum[:, :], 1.0)
            V.memset(rc[:, :], 1.0)
            V.memset(kept[:, :], 1.0)
            V.memset(score[:, :], 0.0)
            V.memset(natt[:, :], 0.0)
            V.memset(below[:, N:N + PAD], 0.0)
            for k in range(HALVINGS + 1):
                V.memset(factor[:, k:k + 1], float(np.exp(SPAN / 2 ** (k + 1))))
            fence()

            dve.wait_ge(x_in, 32)
            for t in range(NT):
                V.bn_stats(stats[0:rows(t), t, :], E[0:rows(t), t, 0:D])
            fence()
            for t in range(NT):
                V.bn_aggr(mv[0:rows(t), t, :], stats[0:rows(t), t, :])
            fence()
            inverse_roots(0)

            for t in range(NT):
                r = rows(t)
                dve.wait_ge(h_turned, t + 1)
                src = ps[:, 6 + t % 2, 0:D].rearrange("p (c r) -> p c r", c=DC)[:, :, 0:r]
                V.tensor_copy(hT[:, :, nodes(t)], src).then_inc(hT_ready, 1)

            def logits_of(t):
                return ps[:, 3 * (t % 2):3 * (t % 2) + NB, :].rearrange("p b n -> p (b n)")[:, 0:N]

            def keys(s):
                dve.wait_ge(qk_done, 3 * s + 2)
                for b in range(NB):
                    n = N - BANK * b if b == NB - 1 else BANK
                    i = V.tensor_copy(KT[:, chunk(b)], ps[0:H, NB + b, 0:n])
                i.then_inc(qk_copied, 1)

            def maxima(s):
                for t in range(NT):
                    r = rows(t)
                    dve.wait_ge(logits_done, s * NT + t + 1)
                    V.tensor_reduce(nmax[0:r, t:t + 1], logits_of(t)[0:r, :], AX.X, ALU.max, negate=True)
                    V.drain().then_inc(max_ready, 1)

            def halve(k):
                for t in range(NT):
                    r = rows(t)
                    V.scalar_tensor_tensor(below[0:r, 0:N], E[0:r, t, :], mid[0:r, t:t + 1], E[0:r, t, :],
                                           ALU.is_ge, ALU.mult, accum_out=mass[0:r, t:t + 1])
                    fence()
                V.tensor_tensor(reached[:, :], mass[:, :], goal[:, :], ALU.is_ge)
                fence()
                V.tensor_tensor(lo_c[:, :], mid[:, :], reached[:, :], ALU.mult)
                V.scalar_tensor_tensor(hi_c[:, :], reached[:, :], HUGE, mid[:, :], ALU.mult, ALU.add)
                V.scalar_tensor_tensor(mass_c[:, :], reached[:, :], -HUGE, mass[:, :], ALU.mult, ALU.add)
                fence()
                V.tensor_tensor(lo[:, :], lo[:, :], lo_c[:, :], ALU.max)
                V.tensor_tensor(hi[:, :], hi[:, :], hi_c[:, :], ALU.min)
                V.tensor_tensor(mass_hi[:, :], mass_hi[:, :], mass_c[:, :], ALU.max)
                fence()
                V.tensor_scalar(mid[:, :], lo[:, :], factor[:, k], None, ALU.mult)
                fence()

            def bracket(s):
                dve.wait_ge(exp_done, (s + 1) * NT)
                V.tensor_scalar(goal[:, :], tot[:, :], P_NUC, None, ALU.mult)
                V.memset(lo[:, :], LOWEST)
                V.memset(hi[:, :], 2.0)
                V.memset(mass_hi[:, :], 0.0)
                V.memset(mid[:, :], float(LOWEST * np.exp(SPAN / 2)))
                fence()
                halve(slice(1, 2))
                if s == 0:
                    dve.wait_ge(csum_done, 1)
                    dve.wait_ge(rsum_done, 1)
                    V.tensor_copy(rc[:, 0:FULL], ps[:, 6, 0:FULL])
                    V.tensor_copy(rc[0:TAIL, FULL:NT], ps[0:TAIL, 6, FULL:NT])
                    V.tensor_scalar(t1[:, :], csum[:, :], 1e-12, None, ALU.max)
                    fence()
                    V.tensor_scalar(t0[:, :], rc[:, :], 1e-12, None, ALU.max)
                    V.reciprocal(inv_c[:, :], t1[:, :])
                    fence()
                    V.reciprocal(inv_r[:, :], t0[:, :])
                    V.drain().then_inc(inv_ready, 1)
                with V.Fori(2, HALVINGS + 1) as k:
                    halve(bass.ds(k, 1))

            def round_counts(s):
                V.reciprocal(t0[:, :], lo[:, :])
                V.tensor_tensor(t1[:, :], goal[:, :], mass_hi[:, :], ALU.subtract)
                fence()
                V.tensor_tensor(t0[:, :], t0[:, :], t1[:, :], ALU.mult)
                fence()
                for sl, q in ((slice(0, P), slice(0, FULL)), (slice(0, TAIL), slice(FULL, NT))):
                    V.tensor_scalar(need[sl, q], t0[sl, q], 1.0 / 8, 1.51, ALU.mult, ALU.add)
                fence()
                V.drain().then_inc(need_ready, 1)
                dve.wait_ge(need_turned, s + 1)
                V.reduce_max(rounds_f[:, :], ps[0:NT, 7, 0:P], axis=AX.X)
                fence()
                V.tensor_scalar(rounds_f[:, :], rounds_f[:, :], MAX_ROUNDS, 1.0, ALU.min, ALU.max)
                fence()
                V.tensor_copy(rounds_i[:, :], rounds_f[:, :])
                fence()

            def take(s, count):
                for t in range(NT):
                    r = rows(t)
                    V.scalar_tensor_tensor(below[0:r, 0:N], E[0:r, t, :], hi[0:r, t:t + 1], E[0:r, t, :],
                                           ALU.is_lt, ALU.mult)
                    V.tensor_copy(cum[0:r, 8:9], mass_hi[0:r, t:t + 1])
                    V.reg_load(count, rounds_i[t:t + 1, 0:1])
                    fence()
                    with V.Fori(0, count):
                        V.max(out=top[0:r, :], in_=below[0:r, :])
                        V.tensor_copy(cum[0:r, 0:1], cum[0:r, 8:9])
                        fence()
                        V.tensor_tensor_scan(cum[0:r, 1:9], top[0:r, :], zero8[0:r, :], cum[0:r, 0:1],
                                             ALU.add, ALU.add)
                        fence()
                        V.scalar_tensor_tensor(taken[0:r, :], cum[0:r, 0:8], goal[0:r, t:t + 1], top[0:r, :],
                                               ALU.is_lt, ALU.mult)
                        fence()
                        V.match_replace(out=below[0:r, :], in_to_replace=taken[0:r, :], in_values=below[0:r, :],
                                        imm_value=0.0)
                        fence()
                    V.scalar_tensor_tensor(E[0:r, t, :], below[0:r, 0:N], -1.0, E[0:r, t, :], ALU.mult, ALU.add,
                                           accum_out=kept[0:r, t:t + 1])
                    V.drain().then_inc(A_ready, 1)
                    V.reciprocal(rkept[0:r, t:t + 1], kept[0:r, t:t + 1])
                    if t >= 1:
                        attended(s, t - 1)
                fence()
                attended(s, NT - 1)

            def attended(s, t):
                r, b = rows(t), t % 2
                dve.wait_ge(ax_done, s * NT + t + 1)
                if s == 0:
                    dve.wait_ge(sx_done, 2 * NT)
                    V.tensor_scalar(Xa[0:r, t, :], ps[0:r, 6 + b, 0:D], rkept[0:r, t:t + 1], None,
                                    ALU.mult).then_inc(xa_ready, 1)
                else:
                    if t >= 2:
                        dve.wait_ge(xa_turned, s * NT + t - 1)
                    V.tensor_scalar(FB2[0:r, b, 0:D], ps[0:r, 6 + b, 0:D], rkept[0:r, t:t + 1], None,
                                    ALU.mult).then_inc(xa_ready, 1)

            count = V.alloc_register("rounds")
            for s in range(2):
                keys(s)
                maxima(s)
                bracket(s)
                round_counts(s)
                take(s, count)

            for t in range(NT):
                dve.wait_ge(y_ready, t + 1)
                V.bn_stats(stats[0:rows(t), t, :], Z[0:rows(t), t, :])
            fence()
            for t in range(NT):
                V.bn_aggr(mv[0:rows(t), t, :], stats[0:rows(t), t, :])
            fence()
            inverse_roots(1)
            fence()
            dve.wait_ge(sp_in, 16 * 8)
            for t in range(NT):
                r = rows(t)
                V.tensor_scalar(Z[0:r, t, :], Z[0:r, t, :], rstd[0:r, t:t + 1], nmr[0:r, t:t + 1], ALU.mult, ALU.add)
            fence()
            for t in range(NT):
                r = rows(t)
                V.tensor_tensor(Z[0:r, t, :], Z[0:r, t, :], gam[0:r, :], ALU.mult)
                V.tensor_tensor(xres[0:r, t, :], xres[0:r, t, :], bet[0:r, :], ALU.add)
            fence()
            for t in range(NT):
                r = rows(t)
                V.tensor_tensor(Z[0:r, t, :], Z[0:r, t, :], xres[0:r, t, :], ALU.add)
            fence()
            for t in range(NT):
                V.bn_stats(stats[0:rows(t), t, :], Z[0:rows(t), t, :])
            fence()
            for t in range(NT):
                V.bn_aggr(mv[0:rows(t), t, :], stats[0:rows(t), t, :])
            V.drain().then_inc(x1_ready, NT)
            inverse_roots(2)
            dve.wait_ge(sup_ready, NT)
            V.tensor_copy(score[:, 0:FULL], support[:, 0:FULL, D])
            V.tensor_copy(score[:, FULL:NT], support[:, 0, D:D + 1])
            fence()
            V.tensor_copy(score[0:TAIL, FULL:NT], support[0:TAIL, FULL, D:D + 1])
            fence()
            V.reduce_max(nmx[:, :], score[:, :], axis=AX.X)
            V.drain().then_inc(score_max, 1)
            dve.wait_ge(score_max, 2)
            V.tensor_reduce(nall[0:1, :], ps[0:1, 7, 0:P], AX.X, ALU.max, negate=True)
            V.drain().then_inc(score_max, 1)
            dve.wait_ge(score_max, 4)
            V.tensor_copy(nall[:, :], ps[:, 7, 0:1])
            V.drain().then_inc(score_all, 1)
            dve.wait_ge(score_exp, 1)
            V.reduce_sum(ncol[:, :], natt[:, :], axis=AX.X)
            V.drain().then_inc(score_sum, 1)
            dve.wait_ge(score_tot, 1)
            V.reciprocal(ntot[:, :], ps[:, 7, 0:1])
            fence()
            V.tensor_scalar(natt[:, :], natt[:, :], ntot[:, 0:1], None, ALU.mult)
            V.drain().then_inc(score_all, 1)

            for t in range(NT + 3):
                if t < NT:
                    r, b = rows(t), t % 2
                    dve.wait_ge(e_done, t + 1)
                    dve.wait_ge(negm_ready, t + 1)
                    if t >= 2:
                        dve.wait_ge(pa_turned, t - 1)
                    V.tensor_tensor_reduce(out=em[0:r, b, :], in0=logits_of(t)[0:r, :], in1=negm[0:r, b, :],
                                           scale=1.0, scalar=-3.0e38, op0=ALU.add, op1=ALU.max,
                                           accum_out=psum_max[0:r, t:t + 1])
                    fence()
                    V.tensor_scalar(nm1[0:r, t:t + 1], psum_max[0:r, t:t + 1], -1.0, None, ALU.mult)
                    V.drain().then_inc(em_ready, 1)
                if 1 <= t <= NT:
                    u = t - 1
                    r, b = rows(u), u % 2
                    dve.wait_ge(p_ready, u + 1)
                    V.tensor_tensor(em[0:r, b, :], em[0:r, b, :], adj_n[0:r, u, :], ALU.mult).then_inc(pa_ready, 1)
                    V.reciprocal(rkept[0:r, u:u + 1], psum_row[0:r, u:u + 1])
                    fence()
                    V.tensor_tensor(final[0:r, u:u + 1], rkept[0:r, u:u + 1], natt[0:r, u:u + 1], ALU.mult)
                if t >= 3:
                    u = t - 3
                    r, b = rows(u), u % 2
                    dve.wait_ge(out_sum, u + 1)
                    dve.wait_ge(xb_ready, u + 1)
                    V.scalar_tensor_tensor(Z[0:r, u, :], ps[0:r, 6 + b, 0:D], final[0:r, u:u + 1], Z[0:r, u, :],
                                           ALU.mult, ALU.add).then_inc(out_ready, 1)

        @block.tensor
        def _(pe):
            T = nc.tensor

            def turn(dst, src, r):
                return T.transpose(dst, src, ident[0:r, 0:r])

            pe.wait_ge(const_ready, 3)
            for t in range(NT):
                r, b = rows(t), t % 2
                pe.wait_ge(h_ready, t + 1)
                if t >= 2:
                    pe.wait_ge(hT_ready, t - 1)
                for c in range(DC):
                    i = turn(ps[:, 6 + b, c * P:c * P + r], h[0:r, t, c * P:(c + 1) * P], r)
                i.then_inc(h_turned, 1)

            def projections(s, XT):
                if s == 0:
                    pe.wait_ge(hT_ready, NT)
                    pe.wait_ge(w_in, 48)
                else:
                    pe.wait_ge(xaT_ready, NT)
                    pe.wait_ge(AT_ready, NT)
                for base, W in ((0, W1s), (NB, W3s)):
                    for b in range(NB):
                        n = N - BANK * b if b == NB - 1 else BANK
                        for c in range(DC):
                            i = T.matmul(ps[0:H, base + b, 0:n], W[:, c, :], XT[:, c, chunk(b)],
                                         start=(c == 0), stop=(c == DC - 1))
                    i.then_inc(qk_done, 1)
                pe.wait_ge(qk_copied, 3 * s + 2)
                for b in range(NB):
                    n = N - BANK * b if b == NB - 1 else BANK
                    i = T.matmul(ps[0:H, b, 0:n], W2s[:, :], QT[:, chunk(b)], start=True, stop=True)
                i.then_inc(qk_done, 1)

            def logits(s):
                pe.wait_ge(qk_copied, 3 * s + 3)
                for t in range(NT):
                    r = rows(t)
                    if t >= 2:
                        pe.wait_ge(exp_done, s * NT + t - 1)
                    for b in range(NB):
                        n = N - BANK * b if b == NB - 1 else BANK
                        i = T.matmul(ps[0:r, 3 * (t % 2) + b, 0:n], Q2T[:, nodes(t)], KT[:, chunk(b)],
                                     start=True, stop=True)
                    i.then_inc(logits_done, 1)

            def diffusion(s):
                for t in range(NT + 2):
                    if t < NT:
                        r, b = rows(t), t % 2
                        if s * NT + t >= 2:
                            pe.wait_ge(fb_ready, s * NT + t - 1)
                        if s == 1 and t == 0:
                            pe.wait_ge(fb_ready, NT)
                        for k in range(NT):
                            q = rows(k)
                            rhs = h[0:q, k, :] if s == 0 else FB[0:q, k, :]
                            i = T.matmul(ps[0:r, b, 0:(1 + s) * D], ST[0:q, k, nodes(t)], rhs,
                                         start=(k == 0), stop=(k == NT - 1))
                        i.then_inc(sx_done, 1)
                    if 1 <= t <= NT:
                        u = t - 1
                        r, b = rows(u), u % 2
                        pe.wait_ge(fb_ready, s * NT + u + 1)
                        if s * NT + u >= 2:
                            pe.wait_ge(fbT_ready, s * NT + u - 1)
                        src = FB[0:r, u, :] if s == 0 else FB2[0:r, b, :]
                        for c in range(2 * DC):
                            i = turn(ps[:, 2 + b, c * P:c * P + r], src[:, c * P:(c + 1) * P], r)
                        i.then_inc(fb_turned, 1)
                    if t >= 2:
                        u = t - 2
                        r, b = rows(u), u % 2
                        pe.wait_ge(fbT_ready, s * NT + u + 1)
                        if s * NT + u >= 2:
                            pe.wait_ge(z_ready, s * NT + u - 1)
                        if s == 1:
                            pe.wait_ge(z_ready, u + 1)
                        T.matmul(ps[0:r, 4 + b, 0:D], ident[0:r, 0:r], h[0:r, u, :] if s == 0 else Z[0:r, u, :],
                                 start=True, stop=False)
                        for d in range(2):
                            for c in range(DC):
                                k = d * DC + c
                                i = T.matmul(ps[0:r, 4 + b, 0:D], turned[:, b, k * P:k * P + r],
                                             U12[:, s, d, c, :], start=False, stop=(k == 2 * DC - 1))
                        i.then_inc(z_done, 1)

            def attend(s):
                for t in range(NT + 2):
                    g = s * NT + t
                    if t < NT:
                        r, b = rows(t), t % 2
                        pe.wait_ge(A_ready, g + 1)
                        if t >= 2:
                            pe.wait_ge(AT_ready, g - 1)
                        for j in range(NT):
                            i = turn(ps[0:rows(j), 3 * b + j // TB, (j % TB) * P:(j % TB) * P + r],
                                     E[0:r, t, nodes(j)], r)
                        i.then_inc(A_turned, 1)
                    if 1 <= t <= NT:
                        u = t - 1
                        r, b = rows(u), u % 2
                        pe.wait_ge(AT_ready, s * NT + u + 1)
                        if u >= 2:
                            pe.wait_ge(xaT_ready, s * NT + u - 1)
                            if s == 1:
                                pe.wait_ge(y_ready, u - 1)
                        X = h if s == 0 else Xa
                        for j in range(NT):
                            q = rows(j)
                            i = T.matmul(ps[0:r, 6 + b, 0:D], AT[0:q, b, j, 0:r], X[0:q, j, :],
                                         start=(j == 0), stop=(j == NT - 1))
                        i.then_inc(ax_done, 1)
                    if t >= 2:
                        u = t - 2
                        r, b = rows(u), u % 2
                        pe.wait_ge(xa_ready, s * NT + u + 1)
                        src = Xa[0:r, u, :] if s == 0 else FB2[0:r, b, 0:D]
                        for c in range(DC):
                            i = turn(ps[:, 6 + b, D + c * P:D + c * P + r], src[:, c * P:(c + 1) * P], r)
                        i.then_inc(xa_turned, 1)
                        if s == 1:
                            pe.wait_ge(xaT_ready, NT + u + 1)
                            T.matmul(ps[0:r, 6 + b, 0:D], ident[0:r, 0:r], Z[0:r, u, :], start=True, stop=False)
                            for c in range(DC):
                                T.matmul(ps[0:r, 6 + b, 0:D], XaT[:, c, nodes(u)], U3s[:, 0, c, :],
                                         start=False, stop=False)
                            for c in range(DC):
                                i = T.matmul(ps[0:r, 6 + b, 0:D], turned[:, b, c * P:c * P + r], U3s[:, 1, c, :],
                                             start=False, stop=(c == DC - 1))
                            i.then_inc(y_done, 1)

            def turn_needs(s):
                pe.wait_ge(need_ready, s + 1)
                turn(ps[0:NT, 7, 0:P], need[:, :], P).then_inc(need_turned, 1)

            projections(0, hT)
            logits(0)
            pe.wait_ge(csum_done, 1)
            for t in range(NT):
                for k in range(NT):
                    q = rows(k)
                    i = T.matmul(ps[0:rows(t), 6, t:t + 1], ST[0:q, k, nodes(t)], ones[0:q, :],
                                 start=(k == 0), stop=(k == NT - 1))
            i.then_inc(rsum_done, 1)
            pe.wait_ge(exp_done, NT)
            pe.wait_ge(u_in, 96)
            diffusion(0)
            diffusion(1)
            pe.wait_ge(z_ready, 2 * NT)
            turn_needs(0)
            attend(0)
            projections(1, XaT)
            logits(1)
            pe.wait_ge(exp_done, 2 * NT)
            turn_needs(1)
            attend(1)

            for t in range(NT):
                r, b = rows(t), t % 2
                pe.wait_ge(h2_ready, t + 1)
                if t >= 2:
                    pe.wait_ge(h2T_ready, t - 1)
                for c in range(DC):
                    i = turn(ps[:, 6 + b, c * P:c * P + r], h[0:r, t, c * P:(c + 1) * P], r)
                i.then_inc(h2_turned, 1)
            pe.wait_ge(h2T_ready, NT)
            pe.wait_ge(sp_in, 128)
            for m in range(DC):
                for b in range(NB):
                    n = N - BANK * b if b == NB - 1 else BANK
                    for c in range(DC):
                        i = T.matmul(ps[:, 3 * m + b, 0:n], EW[:, c, m * P:(m + 1) * P], h2T[:, c, chunk(b)],
                                     start=(c == 0), stop=(c == DC - 1))
                i.then_inc(hh_done, 1)
            for t in range(NT):
                r, b = rows(t), t % 2
                if t >= 2:
                    pe.wait_ge(sup_ready, t - 1)
                for c in range(DC):
                    i = T.matmul(ps[0:r, 6 + b, 0:D + 1], h2T[:, c, nodes(t)], WN[:, c, :],
                                 start=(c == 0), stop=(c == DC - 1))
                i.then_inc(sup_done, 1)

            def edges(t):
                r = rows(t)
                if t >= 2:
                    pe.wait_ge(em_ready, t - 1)
                    pe.wait_ge(paT_ready, t - 1)
                for b in range(NB):
                    n = N - BANK * b if b == NB - 1 else BANK
                    for c in range(DC):
                        i = T.matmul(ps[0:r, 3 * (t % 2) + b, 0:n], hhT[:, c, nodes(t)], hhT[:, c, chunk(b)],
                                     start=(c == 0), stop=(c == DC - 1))
                i.then_inc(e_done, 1)

            pe.wait_ge(score_max, 1)
            turn(ps[0:1, 7, 0:P], nmx[:, :], P).then_inc(score_max, 1)
            pe.wait_ge(score_max, 3)
            T.matmul(ps[:, 7, 0:1], ones_row, nall[0:1, :], start=True, stop=True).then_inc(score_max, 1)
            pe.wait_ge(hhT_ready, DC)
            edges(0)
            pe.wait_ge(score_sum, 1)
            T.matmul(ps[:, 7, 0:1], ones_all[:, :], ncol[:, :], start=True, stop=True).then_inc(score_tot, 1)
            pe.wait_ge(score_all, 2)
            for t in range(NT + 1):
                if t + 1 < NT:
                    edges(t + 1)
                if t < NT:
                    r, b = rows(t), t % 2
                    pe.wait_ge(pa_ready, t + 1)
                    for j in range(NT):
                        i = turn(ps[0:rows(j), 3 * b + j // TB, (j % TB) * P:(j % TB) * P + r],
                                 em[0:r, b, nodes(j)], r)
                    i.then_inc(pa_turned, 1)
                if t >= 1:
                    u = t - 1
                    r, b = rows(u), u % 2
                    pe.wait_ge(paT_ready, u + 1)
                    if u >= 2:
                        pe.wait_ge(out_ready, u - 1)
                    for j in range(NT):
                        q = rows(j)
                        i = T.matmul(ps[0:r, 6 + b, 0:D], AT[0:q, b, j, 0:r], support[0:q, j, 0:D],
                                     start=(j == 0), stop=(j == NT - 1))
                    i.then_inc(out_sum, 1)


_INS = ['x', 'adj', 'adj_t', 'L0_gnn_W1', 'L0_gnn_W2', 'L0_gnn_W3', 'L0_gnn_U1', 'L0_gnn_U2', 'L0_gnn_U3',
        'L0_gnn_gamma', 'L0_gnn_beta', 'L1_gnn_weight', 'L1_gnn_bias', 'L1_gnn_node_w', 'L1_gnn_edge_w']


def kernel(**inputs):
    import numpy as _np
    import concourse.bacc as _bacc
    from concourse import mybir as _mybir
    from concourse.bass_utils import run_bass_kernel_spmd as _run

    nc = _bacc.Bacc("TRN2", target_bir_lowering=False, num_devices=1)
    laid_out = dict(inputs, adj_t=_np.asarray(inputs['adj']).T)
    arrays, args = {}, []
    for name in _INS:
        a = _np.ascontiguousarray(laid_out[name])
        arrays[f"in_{name}_dram"] = a
        args.append(nc.dram_tensor(f"in_{name}_dram", a.shape, _mybir.dt.from_np(a.dtype), kind="ExternalInput").ap())
    y = nc.dram_tensor("out_0_dram", inputs['x'].shape, _mybir.dt.float32, kind="ExternalOutput").ap()
    gnn_block(nc, *args, y)
    r = _run(nc, [arrays], core_ids=[0])
    return r.results[0]["out_0_dram"]
```

```python
from contextlib import ExitStack

import concourse.bass as bass
from concourse import mybir

F32 = mybir.dt.float32
BF16 = mybir.dt.bfloat16
I32 = mybir.dt.int32
ALU = mybir.AluOpType
ACT = mybir.ActivationFunctionType
AX = mybir.AxisListType

P = 128
P_NUC = 0.9
LN_EPS = 1e-5
NEG_BIG = -9.0e15
HUGE = 1.0e30
HALVINGS = (6, 7)


def gnn_block(nc, x, adj, adj_t, W1, W2, W3, U1, U2, U3, gamma, beta, weight, bias, node_w, edge_w, out):
    N, D = x.shape
    H = W1.shape[1]
    NT = -(-N // P)
    FULL = N // P
    TAIL = N - FULL * P
    DC = D // P
    BANK = 512
    NB = -(-N // BANK)
    TB = BANK // P
    PAD = 8
    assert DC == 2 and NT == FULL + 1 and TAIL > 0 and NB == 3 and H <= P and 2 * D == BANK

    SHARED = 3
    OWN = NT - SHARED

    LOWEST = (1.0 - P_NUC) / N * 0.999
    MAX_ROUNDS = float(-(-N // 8))

    def rows(t):
        return P if t < FULL else TAIL

    def nodes(t):
        return slice(t * P, t * P + rows(t))

    def bank_of(b):
        return slice(b * BANK, min(N, (b + 1) * BANK))

    def bank_len(b):
        return min(N, (b + 1) * BANK) - b * BANK

    with ExitStack() as ctx:
        def sb(name, shape, dt=F32):
            return ctx.enter_context(nc.sbuf_tensor(name, shape, dt))

        def sem(name):
            return ctx.enter_context(nc.semaphore(name))

        reg_adj = sb("reg_adj", [P, NT, N])
        reg_rows = sb("reg_rows", [P, NT, N])
        reg_h = sb("reg_h", [P, NT, D + 1])
        reg_mix = sb("reg_mix", [P, NT * 2 * D])
        reg_t = sb("reg_t", [P, DC, N])
        reg_z = sb("reg_z", [P, NT * D])
        reg_at = sb("reg_at", [P, 2, NT * P])
        reg_u = sb("reg_u", [P, 2, DC, 2, D])
        below = sb("below", [P, N + PAD])
        unused = sb("unused", [P, N], BF16)

        ST = reg_adj
        E = reg_rows
        h = reg_h[:, :, 0:D]
        hT = reg_t
        XaT = reg_t
        Z = reg_z[:, :].rearrange("p (t d) -> p t d", t=NT)
        FB = reg_mix[:, :].rearrange("p (t d) -> p t d", t=NT)
        h2T = reg_mix[:, 0:DC * N].rearrange("p (c n) -> p c n", c=DC)
        hhT = reg_mix[:, NT * D:NT * D + DC * N].rearrange("p (c n) -> p c n", c=DC)
        AT = reg_at[:, :, :].rearrange("p b (j r) -> p b j r", j=NT)
        Q2T = reg_at[0:H, 0, 0:N]
        KT = reg_at[0:H, 1, 0:N]
        QT = below[0:H, 0:N]
        GT = reg_at[:, 0, 0:2 * D].rearrange("p (b d) -> p b d", b=2)
        share = reg_at[:, 1, 0:4 * D].rearrange("p (b d) -> p b d", b=2)
        U12 = reg_u
        xa = reg_u[:, 0, 0, :, :]
        spare = reg_rows[:, 0:5, :].rearrange("p t n -> p (t n)")
        xres = spare[:, 0:NT * D].rearrange("p (t d) -> p t d", t=NT)
        o = NT * D
        gam, bet, bia = (spare[:, o + i * D:o + (i + 1) * D] for i in range(3))
        o += 3 * D
        EW = spare[:, o:o + DC * D].rearrange("p (c d) -> p c d", c=DC)
        o += DC * D
        WN = spare[:, o:o + DC * (D + 1)].rearrange("p (c d) -> p c d", c=DC)
        assert o + DC * (D + 1) <= 5 * N
        adj_n = reg_adj
        support = reg_h
        negm = reg_rows[:, 5:7, :]
        em = reg_rows[:, 7:9, :]

        W1s = sb("W1s", [P, DC, H])
        W3s = sb("W3s", [P, DC, H])
        W2s = sb("W2s", [H, H])
        U3s = sb("U3s", [P, DC, 2, D])
        ident = sb("ident", [P, P])
        ones_all = sb("ones_all", [P, P])
        ones_row = ones_all[0:1, :]

        (var, sd, rstd, t0, t1, nmr, nmax, tot, goal, mid, mass, reached, lo, hi, mass_hi, lo_c, hi_c, mass_c,
         need, kept, rkept, csum, inv_c, inv_r, nm1, edge_max, edge_sum, score, natt, final, neg_span) = (
            sb(n, [P, NT]) for n in (
                "var", "sd", "rstd", "t0", "t1", "nmr", "nmax", "tot", "goal", "mid", "mass", "reached", "lo", "hi",
                "mass_hi", "lo_c", "hi_c", "mass_c", "need", "kept", "rkept", "csum", "inv_c", "inv_r", "nm1",
                "edge_max", "edge_sum", "score", "natt", "final", "neg_span"))
        relu_sum, sign_sum, neg_mid = (sb(n, [P, SHARED]) for n in ("relu_sum", "sign_sum", "neg_mid"))
        nmx, nall, ncol, ntot = (sb(n, [P, 1]) for n in ("nmx", "nall", "ncol", "ntot"))
        stats = sb("stats", [P, NT, 6])
        mv = sb("mv", [P, NT, 2])
        factor = sb("factor", [P, max(HALVINGS) + 1, NT])
        rounds_f = sb("rounds_f", [NT, 1])
        rounds_i = sb("rounds_i", [NT, 1], I32)
        top = sb("top", [P, 8])
        taken = sb("taken", [P, 8])
        zero8 = sb("zero8", [P, 8])
        cum = sb("cum", [P, 9])

        ps = ctx.enter_context(nc.psum_tensor("ps", [P, 8, BANK], F32))

        x_in, w_in, u_in, st_in, sp_in, adj_in, out_done = (
            sem(n) for n in ("x_in", "w_in", "u_in", "st_in", "sp_in", "adj_in", "out_done"))
        st_diag, const_ready = sem("st_diag"), sem("const_ready")
        var_ready, sd_ready, norm_ready = sem("var_ready"), sem("sd_ready"), sem("norm_ready")
        h_ready, h_turned, hT_ready = sem("h_ready"), sem("h_turned"), sem("hT_ready")
        qk_done, q_copied, k_copied, q2_copied = (sem(n) for n in ("qk_done", "q_copied", "k_copied", "q2_copied"))
        logits_done, max_ready, exp_done = sem("logits_done"), sem("max_ready"), sem("exp_done")
        factor_ready, mid_ready, shared_mass = sem("factor_ready"), sem("mid_ready"), sem("shared_mass")
        sx_done, sx_ready, csum_done, inv_ready = sem("sx_done"), sem("sx_ready"), sem("csum_done"), sem("inv_ready")
        g_turned, gT_ready, gu_done, gu_ready = sem("g_turned"), sem("gT_ready"), sem("gu_done"), sem("gu_ready")
        x3_done, x3_ready, sv_done, sv_ready = sem("x3_done"), sem("x3_ready"), sem("sv_done"), sem("sv_ready")
        share_added = sem("share_added")
        need_ready, need_turned = sem("need_ready"), sem("need_turned")
        A_ready, A_turned, AT_ready, kept_ready = sem("A_ready"), sem("A_turned"), sem("AT_ready"), sem("kept_ready")
        ax_done, xa_ready, xa_turned, xaT_ready = sem("ax_done"), sem("xa_ready"), sem("xa_turned"), sem("xaT_ready")
        y_ready = sem("y_ready")
        xbeta_ready, yn_ready, yg_ready, h2_ready, xb_ready = (
            sem(n) for n in ("xbeta_ready", "yn_ready", "yg_ready", "h2_ready", "xb_ready"))
        h2_turned, h2T_ready, hh_done, hhT_ready = sem("h2_turned"), sem("h2T_ready"), sem("hh_done"), sem("hhT_ready")
        sup_done, sup_ready = sem("sup_done"), sem("sup_ready")
        negm_ready, e_done, em_ready, p_ready, pa_ready = (
            sem(n) for n in ("negm_ready", "e_done", "em_ready", "p_ready", "pa_ready"))
        pa_turned, paT_ready, out_sum, out_ready = (
            sem(n) for n in ("pa_turned", "paT_ready", "out_sum", "out_ready"))
        score_max, score_turned, score_top, score_spread, score_all, score_exp, score_sum, score_tot, natt_ready = (
            sem(n) for n in ("score_max", "score_turned", "score_top", "score_spread", "score_all", "score_exp",
                             "score_sum", "score_tot", "natt_ready"))

        def logits_of(t):
            return ps[:, 3 * (t % 2):3 * (t % 2) + NB, :].rearrange("p b n -> p (b n)")[:, 0:N]

        def turned_features(bank, col, r):
            return ps[:, bank, col:col + D].rearrange("p (c r) -> p c r", c=DC)[:, :, 0:r]

        block = ctx.enter_context(nc.Block())

        @block.sync
        def _(sp):
            sp.dma_start(E[:, 0:FULL, 0:D], x[0:FULL * P, :].rearrange("(t p) d -> p t d", p=P)).then_inc(x_in, 16)
            sp.dma_start(E[0:TAIL, FULL, 0:D], x[FULL * P:N, :]).then_inc(x_in, 16)
            sp.dma_start(W1s[:, :, :], W1.rearrange("(c p) n -> p c n", p=P)).then_inc(w_in, 16)
            sp.dma_start(W3s[:, :, :], W3.rearrange("(c p) n -> p c n", p=P)).then_inc(w_in, 16)
            sp.dma_start(W2s[:, :], W2).then_inc(w_in, 16)
            for k in range(NT):
                sp.dma_start(ST[0:rows(k), k, :], adj_t[nodes(k), :]).then_inc(st_in, 16)
            for s in range(2):
                for dst, U in ((U12[:, 0, :, s, :], U1), (U12[:, 1, :, s, :], U2), (U3s[:, :, s, :], U3)):
                    sp.dma_start(dst, U[s, :, :].rearrange("(c p) n -> p c n", p=P)).then_inc(u_in, 16)
            sp.wait_ge(sv_done, NT)
            for t in range(NT):
                sp.dma_start(adj_n[0:rows(t), t, :], adj[nodes(t), :]).then_inc(adj_in, 16)
            sp.wait_ge(A_turned, NB * (NT + 5))
            sp.dma_start(xres[:, 0:FULL, :], x[0:FULL * P, :].rearrange("(t p) d -> p t d", p=P)).then_inc(sp_in, 16)
            sp.dma_start(xres[0:TAIL, FULL, :], x[FULL * P:N, :]).then_inc(sp_in, 16)
            for dst, src in ((gam, gamma), (bet, beta), (bia, bias)):
                sp.dma_start(dst, src.partition_broadcast(P)).then_inc(sp_in, 16)
            sp.dma_start(EW, edge_w.rearrange("(c p) n -> p c n", p=P)).then_inc(sp_in, 16)
            sp.dma_start(WN[:, :, 0:D], weight.rearrange("(c p) n -> p c n", p=P)).then_inc(sp_in, 16)
            with nc.allow_non_contiguous_dma(reason="node_w is one column of a few hundred values"):
                sp.dma_start(WN[:, :, D:D + 1], node_w.rearrange("(c p) n -> p c n", p=P)).then_inc(sp_in, 16)
            for t in range(NT):
                sp.wait_ge(out_ready, t + 1)
                sp.dma_start(out[nodes(t), :], Z[0:rows(t), t, :]).then_inc(out_done, 16)
            sp.wait_ge(out_done, 16 * NT)

        @block.gpsimd
        def _(pool):
            G = nc.gpsimd
            G.memset(ident[:, :], 0.0).then_inc(const_ready, 1)
            G.memset(ones_all[:, :], 1.0).then_inc(const_ready, 1)
            pool.wait_ge(const_ready, 2)
            G.affine_select(out=ident[:, :], in_=ident[:, :], compare_op=ALU.not_equal, fill=1.0, base=0,
                            pattern=[[-1, P]], channel_multiplier=1).then_inc(const_ready, 1)
            pool.wait_ge(const_ready, 3)
            for k in range(NT):
                r = rows(k)
                pool.wait_ge(st_in, 16 * NT)
                G.tensor_tensor(ST[0:r, k, nodes(k)], ST[0:r, k, nodes(k)], ident[0:r, 0:r],
                                ALU.add).then_inc(st_diag, 1)
            for i in range(3 * NT):
                stage, t = divmod(i, NT)
                r = rows(t)
                pool.wait_ge((gu_ready, x3_ready, sv_ready)[stage], t + 1)
                base = h if stage == 0 else Z
                G.tensor_tensor(Z[0:r, t, :], base[0:r, t, :], share[0:r, i % 2, 0:D], ALU.add)
                if stage != 1:
                    G.drain()
                    G.tensor_tensor(Z[0:r, t, :], Z[0:r, t, :], share[0:r, i % 2, D:2 * D], ALU.add)
                G.drain().then_inc(share_added, 1)
            pool.wait_ge(sp_in, 16 * 8)
            for t in range(NT):
                r = rows(t)
                G.tensor_tensor(xres[0:r, t, :], xres[0:r, t, :], bet[0:r, :], ALU.add).then_inc(xbeta_ready, 1)

            def absent(t):
                r = rows(t)
                if t >= 2:
                    pool.wait_ge(em_ready, t - 1)
                G.tensor_scalar(negm[0:r, t % 2, :], adj_n[0:r, t, :], 0.0, NEG_BIG,
                                ALU.is_le, ALU.mult).then_inc(negm_ready, 1)

            pool.wait_ge(adj_in, 16 * NT)
            pool.wait_ge(A_turned, NB * (NT + 7))
            for t in range(2):
                absent(t)
            for t in range(NT):
                r = rows(t)
                pool.wait_ge(yn_ready, t + 1)
                G.tensor_tensor(Z[0:r, t, :], Z[0:r, t, :], gam[0:r, :], ALU.mult).then_inc(yg_ready, 1)
            for t in range(NT):
                r = rows(t)
                pool.wait_ge(h2_ready, t + 1)
                G.tensor_tensor(Z[0:r, t, :], Z[0:r, t, :], bia[0:r, :], ALU.add).then_inc(xb_ready, 1)
            for t in range(2, NT):
                absent(t)

        @block.scalar
        def _(act):
            A = nc.scalar

            def copy(dst, src):
                return A.activation(dst, src, ACT.Copy)

            def scaled(dst, src, by):
                return A.activation(dst, src, ACT.Copy, scale=by)

            def roots(n):
                act.wait_ge(var_ready, n + 1)
                A.activation(sd[:, :], var[:, :], ACT.Sqrt).then_inc(sd_ready, 1)

            def projections(s):
                for done, dst, copied in ((1, QT, q_copied), (3, Q2T, q2_copied)):
                    act.wait_ge(qk_done, 3 * s + done)
                    for b in range(NB):
                        last = copy(dst[:, bank_of(b)], ps[0:H, b, 0:bank_len(b)])
                    last.then_inc(copied, 1)

            def exps(s):
                for t in range(NT):
                    r = rows(t)
                    act.wait_ge(max_ready, s * NT + t + 1)
                    A.activation(E[0:r, t, :], logits_of(t)[0:r, :], ACT.Exp, bias=nmax[0:r, t:t + 1],
                                 accum_out=tot[0:r, t:t + 1]).then_inc(exp_done, 1)
                A.drain()
                A.activation(neg_span[:, :], tot[:, :], ACT.Ln, scale=LOWEST)
                A.drain()
                for k in range(HALVINGS[s] + 1):
                    A.activation(factor[:, k, :], neg_span[:, :], ACT.Exp, scale=-0.5 ** (k + 1))
                A.drain().then_inc(factor_ready, 1)

            def shared_masses(s, k):
                act.wait_ge(mid_ready, sum(HALVINGS[:s]) + k + 1)
                for q in range(SHARED):
                    t = OWN + q
                    r = rows(t)
                    for func, dst in ((ACT.Relu, relu_sum), (ACT.Sign, sign_sum)):
                        A.activation(unused[0:r, :], E[0:r, t, :], func, bias=neg_mid[0:r, q:q + 1],
                                     accum_out=dst[0:r, q:q + 1])
                        last = A.drain()
                last.then_inc(shared_mass, 1)

            def column_sum(k):
                r = rows(k)
                A.activation(unused[0:r, :], ST[0:r, k, :], ACT.Copy, accum_out=csum[0:r, k:k + 1])
                A.drain().then_inc(csum_done, 1)

            def sx_out(t):
                r = rows(t)
                act.wait_ge(sx_done, t + 1)
                copy(FB[0:r, t, 0:D + 1], ps[0:r, 6 + t % 2, 0:D + 1]).then_inc(sx_ready, 1)

            def share_buffer(i):
                if i >= 2:
                    act.wait_ge(share_added, i - 1)
                return share[:, i % 2, :]

            def gt_out(t):
                act.wait_ge(g_turned, t + 1)
                if t >= 2:
                    act.wait_ge(gu_done, t - 1)
                copy(GT[:, t % 2, :], ps[:, 4 + t % 2, 0:D]).then_inc(gT_ready, 1)

            def gu_out(t):
                r, b = rows(t), t % 2
                act.wait_ge(gu_done, t + 1)
                dst = share_buffer(t)
                for d, inv in enumerate((inv_r, inv_c)):
                    src, by = ps[0:r, 2 * b + d, :], inv[0:r, t:t + 1]
                    scaled(dst[0:r, d * D:(d + 1) * D], src[:, 0:D], by)
                    last = scaled(FB[0:r, t, d * D:(d + 1) * D], src[:, D:2 * D], by)
                last.then_inc(gu_ready, 1)

            def g_out(t):
                if t == 0:
                    act.wait_ge(inv_ready, 1)
                    gt_out(0)
                if t + 1 < NT:
                    gt_out(t + 1)
                gu_out(t)

            def x3_out(t):
                r = rows(t)
                act.wait_ge(x3_done, t + 1)
                dst = share_buffer(NT + t)
                copy(dst[0:r, 0:D], ps[0:r, 6 + t % 2, 0:D])
                copy(h[0:r, t, :], ps[0:r, 6 + t % 2, D:2 * D]).then_inc(x3_ready, 1)

            def sv_out(t):
                r, b = rows(t), (NT + t) % 2
                act.wait_ge(sv_done, t + 1)
                dst = share_buffer(2 * NT + t)
                scaled(dst[0:r, 0:D], ps[0:r, 6 + b, 0:D], inv_r[0:r, t:t + 1])
                scaled(dst[0:r, D:2 * D], ps[0:r, 6 + b, D:2 * D], inv_c[0:r, t:t + 1]).then_inc(sv_ready, 1)

            SUMS = ((0, 1, 2, 3), (4, 5, 6, 7), (8, 9, 10))
            SX = ((0, 1), (2, 3, 4), (5, 6, 7), (8, 9, 10))
            GU = ((), (), (), (), (0, 1, 2), (3, 4, 5))
            X3 = (range(0, 6), range(6, NT))
            SV = ((), (), (0,), (1,), (2, 3), (4,), (5, 6))

            def between(s, k):
                if s == 0:
                    for t in SUMS[k] if k < len(SUMS) else ():
                        column_sum(t)
                    for t in SX[k] if k < len(SX) else ():
                        sx_out(t)
                    for t in GU[k]:
                        g_out(t)
                else:
                    for t in X3[k] if k < len(X3) else ():
                        x3_out(t)
                    for t in SV[k]:
                        sv_out(t)

            def rows_out(base, b, r, turned, ready, n):
                for k in range(NB):
                    act.wait_ge(turned, NB * n + k + 1)
                    j0, j1 = k * TB, min(FULL, (k + 1) * TB)
                    src = ps[:, base + k, :].rearrange("p (j r) -> p j r", j=TB)
                    last = copy(AT[:, b, j0:j1, 0:r], src[:, 0:j1 - j0, 0:r])
                    if k == NB - 1:
                        last = copy(AT[0:TAIL, b, FULL, 0:r], src[0:TAIL, FULL - j0, 0:r])
                    last.then_inc(ready, 1)

            def attend(s):
                act.wait_ge(share_added, NT if s == 0 else 3 * NT)
                for t in range(NT):
                    g = s * NT + t
                    r, b = rows(t), t % 2
                    if g >= 2:
                        act.wait_ge(ax_done, g - 1)
                    rows_out(3 * b, b, r, A_turned, AT_ready, g)
                    if s == 0:
                        if t >= 1:
                            xaT_out(t - 1)
                        act.wait_ge(ax_done, t + 1)
                        act.wait_ge(kept_ready, t + 1)
                        scaled(xa[0:r, b, :], ps[0:r, 6 + b, 0:D], rkept[0:r, t:t + 1]).then_inc(xa_ready, 1)
                if s == 0:
                    xaT_out(NT - 1)

            def xaT_out(t):
                act.wait_ge(xa_turned, t + 1)
                copy(XaT[:, :, nodes(t)], turned_features(6 + t % 2, D, rows(t))).then_inc(xaT_ready, 1)

            roots(0)
            act.wait_ge(norm_ready, 1)
            for t in range(NT):
                r = rows(t)
                A.activation(h[0:r, t, :], E[0:r, t, 0:D], ACT.Relu, bias=nmr[0:r, t:t + 1],
                             scale=rstd[0:r, t:t + 1]).then_inc(h_ready, 1)

            for s in range(2):
                projections(s)
                exps(s)
                if s == 0:
                    act.wait_ge(st_diag, NT)
                for k in range(HALVINGS[s]):
                    shared_masses(s, k)
                    between(s, k)
                if s == 0:
                    for t in range(1 + max(sum(GU, ())), NT):
                        g_out(t)
                else:
                    for t in range(1 + max(sum(SV, ())), NT):
                        sv_out(t)
                attend(s)

            roots(1)
            act.wait_ge(norm_ready, 2)
            for t in range(NT):
                r = rows(t)
                A.activation(Z[0:r, t, :], Z[0:r, t, :], ACT.Identity, bias=nmr[0:r, t:t + 1],
                             scale=rstd[0:r, t:t + 1]).then_inc(yn_ready, 1)
            roots(2)
            act.wait_ge(norm_ready, 3)
            for t in range(NT):
                r = rows(t)
                A.activation(h[0:r, t, :], Z[0:r, t, :], ACT.Relu, bias=nmr[0:r, t:t + 1],
                             scale=rstd[0:r, t:t + 1]).then_inc(h2_ready, 1)
            act.wait_ge(hh_done, 1)
            for b in range(NB):
                last = copy(hhT[:, 0, bank_of(b)], ps[:, b, 0:bank_len(b)])
            last.then_inc(hhT_ready, 1)
            for t in range(NT):
                r = rows(t)
                act.wait_ge(sup_done, t + 1)
                copy(support[0:r, t, :], ps[0:r, 6 + t % 2, 0:D + 1]).then_inc(sup_ready, 1)
            act.wait_ge(score_all, 1)
            A.activation(natt[:, 0:FULL], support[:, 0:FULL, D], ACT.Exp, bias=nall[:, :])
            A.activation(natt[0:TAIL, FULL:NT], support[0:TAIL, FULL, D:D + 1], ACT.Exp,
                         bias=nall[0:TAIL, :]).then_inc(score_exp, 1)
            for t in range(NT + 1):
                if t < NT:
                    r, b = rows(t), t % 2
                    act.wait_ge(em_ready, t + 1)
                    A.activation(em[0:r, b, :], em[0:r, b, :], ACT.Exp, bias=nm1[0:r, t:t + 1],
                                 accum_out=edge_sum[0:r, t:t + 1]).then_inc(p_ready, 1)
                if t >= 1:
                    u = t - 1
                    if u >= 2:
                        act.wait_ge(out_sum, u - 1)
                    rows_out(3, u % 2, rows(u), pa_turned, paT_ready, u)

        @block.vector
        def _(dve):
            V = nc.vector

            def fence():
                V.drain()

            def inverse_roots(n):
                V.tensor_scalar(var[:, :], mv[:, :, 1], LN_EPS, None, ALU.add)
                V.drain().then_inc(var_ready, 1)
                dve.wait_ge(sd_ready, n + 1)
                V.reciprocal(rstd[:, :], sd[:, :])
                fence()
                V.tensor_tensor(t0[:, :], rstd[:, :], rstd[:, :], ALU.mult)
                fence()
                V.tensor_tensor(t0[:, :], t0[:, :], var[:, :], ALU.mult)
                fence()
                V.tensor_scalar(t0[:, :], t0[:, :], -0.5, 1.5, ALU.mult, ALU.add)
                fence()
                V.tensor_tensor(rstd[:, :], rstd[:, :], t0[:, :], ALU.mult)
                fence()
                V.scalar_tensor_tensor(nmr[:, :], mv[:, :, 0], -1.0, rstd[:, :], ALU.mult, ALU.mult)
                V.drain().then_inc(norm_ready, 1)

            def keys(s):
                dve.wait_ge(qk_done, 3 * s + 2)
                for b in range(NB):
                    last = V.tensor_copy(KT[:, bank_of(b)], ps[0:H, NB + b, 0:bank_len(b)])
                last.then_inc(k_copied, 1)

            def maxima(s):
                for t in range(NT):
                    r = rows(t)
                    dve.wait_ge(logits_done, s * NT + t + 1)
                    V.tensor_reduce(nmax[0:r, t:t + 1], logits_of(t)[0:r, :], AX.X, ALU.max, negate=True)
                    V.drain().then_inc(max_ready, 1)

            def halve(s, k):
                V.tensor_scalar(neg_mid[:, :], mid[:, OWN:NT], -1.0, None, ALU.mult)
                V.drain().then_inc(mid_ready, 1)
                for t in range(OWN):
                    V.scalar_tensor_tensor(below[:, 0:N], E[:, t, :], mid[:, t:t + 1], E[:, t, :],
                                           ALU.is_ge, ALU.mult, accum_out=mass[:, t:t + 1])
                    fence()
                dve.wait_ge(shared_mass, sum(HALVINGS[:s]) + k + 1)
                V.scalar_tensor_tensor(t0[:, 0:SHARED], sign_sum[:, :], float(N), mid[:, OWN:NT], ALU.add, ALU.mult)
                fence()
                V.scalar_tensor_tensor(mass[:, OWN:NT], t0[:, 0:SHARED], 0.5, relu_sum[:, :], ALU.mult, ALU.add)
                fence()
                V.tensor_tensor(reached[:, :], mass[:, :], goal[:, :], ALU.is_ge)
                fence()
                V.tensor_tensor(lo_c[:, :], mid[:, :], reached[:, :], ALU.mult)
                V.scalar_tensor_tensor(hi_c[:, :], reached[:, :], HUGE, mid[:, :], ALU.mult, ALU.add)
                V.scalar_tensor_tensor(mass_c[:, :], reached[:, :], -HUGE, mass[:, :], ALU.mult, ALU.add)
                fence()
                V.tensor_tensor(lo[:, :], lo[:, :], lo_c[:, :], ALU.max)
                V.tensor_tensor(hi[:, :], hi[:, :], hi_c[:, :], ALU.min)
                V.tensor_tensor(mass_hi[:, :], mass_hi[:, :], mass_c[:, :], ALU.max)
                fence()
                V.tensor_tensor(mid[:, :], lo[:, :], factor[:, k + 1, :], ALU.mult)
                fence()

            def bracket(s):
                dve.wait_ge(factor_ready, s + 1)
                V.tensor_scalar(goal[:, :], tot[:, :], P_NUC, None, ALU.mult)
                V.tensor_scalar(lo[:, :], tot[:, :], LOWEST, None, ALU.mult)
                V.memset(hi[:, :], 2.0)
                V.memset(mass_hi[:, :], 0.0)
                fence()
                V.tensor_tensor(mid[:, :], lo[:, :], factor[:, 0, :], ALU.mult)
                fence()
                for k in range(HALVINGS[s]):
                    halve(s, k)
                    if s == 0 and k == 3:
                        inverse_sums()
                for t in range(OWN, NT):
                    r = rows(t)
                    V.scalar_tensor_tensor(below[0:r, 0:N], E[0:r, t, :], hi[0:r, t:t + 1], E[0:r, t, :],
                                           ALU.is_gt, ALU.mult, accum_out=mass_hi[0:r, t:t + 1])
                    fence()

            def inverse_sums():
                dve.wait_ge(csum_done, NT)
                dve.wait_ge(sx_ready, NT)
                V.tensor_scalar(t1[:, :], csum[:, :], 1e-12, None, ALU.max)
                V.tensor_scalar(t0[:, 0:FULL], FB[:, 0:FULL, D], 1e-12, None, ALU.max)
                V.tensor_scalar(t0[0:TAIL, FULL:NT], FB[0:TAIL, FULL, D:D + 1], 1e-12, None, ALU.max)
                fence()
                V.reciprocal(inv_c[:, :], t1[:, :])
                V.reciprocal(inv_r[:, 0:FULL], t0[:, 0:FULL])
                V.reciprocal(inv_r[0:TAIL, FULL:NT], t0[0:TAIL, FULL:NT])
                V.drain().then_inc(inv_ready, 1)

            def round_counts(s):
                V.reciprocal(t0[:, :], lo[:, :])
                V.tensor_tensor(t1[:, :], goal[:, :], mass_hi[:, :], ALU.subtract)
                fence()
                V.tensor_tensor(t0[:, :], t0[:, :], t1[:, :], ALU.mult)
                fence()
                for sl, q in ((slice(0, P), slice(0, FULL)), (slice(0, TAIL), slice(FULL, NT))):
                    V.tensor_scalar(need[sl, q], t0[sl, q], 1.0 / 8, 0.501, ALU.mult, ALU.add)
                V.drain().then_inc(need_ready, 1)
                dve.wait_ge(need_turned, s + 1)
                V.reduce_max(rounds_f[:, :], ps[0:NT, 6 if s == 0 else 0, 0:P], axis=AX.X)
                fence()
                V.tensor_scalar(rounds_f[:, :], rounds_f[:, :], MAX_ROUNDS, 1.0, ALU.min, ALU.max)
                fence()
                V.tensor_scalar(rounds_f[:, :], rounds_f[:, :], 2.0 ** 23, None, ALU.add)
                fence()
                V.tensor_scalar(rounds_f[:, :], rounds_f[:, :], 2.0 ** 23, None, ALU.subtract)
                fence()
                V.tensor_copy(rounds_i[:, :], rounds_f[:, :])
                fence()

            def take(s, count):
                for t in range(NT):
                    r = rows(t)
                    V.scalar_tensor_tensor(below[0:r, 0:N], E[0:r, t, :], hi[0:r, t:t + 1], E[0:r, t, :],
                                           ALU.is_lt if t < OWN else ALU.is_le, ALU.mult)
                    V.tensor_copy(cum[0:r, 8:9], mass_hi[0:r, t:t + 1])
                    V.reg_load(count, rounds_i[t:t + 1, 0:1])
                    fence()
                    with V.Fori(0, count):
                        V.max(out=top[0:r, :], in_=below[0:r, :])
                        V.tensor_copy(cum[0:r, 0:1], cum[0:r, 8:9])
                        fence()
                        V.tensor_tensor_scan(cum[0:r, 1:9], top[0:r, :], zero8[0:r, :], cum[0:r, 0:1],
                                             ALU.add, ALU.add)
                        fence()
                        V.scalar_tensor_tensor(taken[0:r, :], cum[0:r, 0:8], goal[0:r, t:t + 1], top[0:r, :],
                                               ALU.is_lt, ALU.mult)
                        fence()
                        V.match_replace(out=below[0:r, :], in_to_replace=taken[0:r, :], in_values=below[0:r, :],
                                        imm_value=0.0)
                        fence()
                    V.scalar_tensor_tensor(E[0:r, t, :], below[0:r, 0:N], -1.0, E[0:r, t, :], ALU.mult, ALU.add,
                                           accum_out=kept[0:r, t:t + 1])
                    V.drain().then_inc(A_ready, 1)
                    V.reciprocal(rkept[0:r, t:t + 1], kept[0:r, t:t + 1]).then_inc(kept_ready, 1)
                    if s == 1 and t >= 2:
                        sum_up(t - 2)
                if s == 1:
                    fence()
                    sum_up(NT - 2)
                    sum_up(NT - 1)

            def sum_up(t):
                r, b = rows(t), t % 2
                if t == 0:
                    dve.wait_ge(share_added, 3 * NT)
                dve.wait_ge(ax_done, NT + t + 1)
                V.scalar_tensor_tensor(Z[0:r, t, :], ps[0:r, 6 + b, 0:D], rkept[0:r, t:t + 1], Z[0:r, t, :],
                                       ALU.mult, ALU.add).then_inc(y_ready, 1)
                fence()
                V.bn_stats(stats[0:r, t, :], Z[0:r, t, :])

            def aggregate():
                fence()
                for t in range(NT):
                    V.bn_aggr(mv[0:rows(t), t, :], stats[0:rows(t), t, :])
                fence()

            for table, value in ((zero8, 0.0), (tot, 1.0), (mass, 0.0), (need, 0.0), (csum, 1.0), (score, 0.0),
                                 (natt, 0.0), (relu_sum, 0.0), (sign_sum, 0.0)):
                V.memset(table[:, :], value)
            V.memset(mv[:, :, :], 1.0)
            V.memset(below[:, N:N + PAD], 0.0)
            V.memset(reg_h[:, :, D:D + 1], 1.0)
            fence()

            dve.wait_ge(x_in, 32)
            for t in range(NT):
                V.bn_stats(stats[0:rows(t), t, :], E[0:rows(t), t, 0:D])
            aggregate()
            inverse_roots(0)
            for t in range(NT):
                dve.wait_ge(h_turned, t + 1)
                V.tensor_copy(hT[:, :, nodes(t)], turned_features(6 + t % 2, 0, rows(t))).then_inc(hT_ready, 1)

            count = V.alloc_register("rounds")
            for s in range(2):
                keys(s)
                maxima(s)
                bracket(s)
                round_counts(s)
                take(s, count)

            aggregate()
            inverse_roots(1)
            dve.wait_ge(xbeta_ready, NT)
            for t in range(NT + 1):
                if t < NT:
                    r = rows(t)
                    dve.wait_ge(yg_ready, t + 1)
                    V.tensor_tensor(Z[0:r, t, :], Z[0:r, t, :], xres[0:r, t, :], ALU.add)
                if t >= 1:
                    V.bn_stats(stats[0:rows(t - 1), t - 1, :], Z[0:rows(t - 1), t - 1, :])
                fence()
            aggregate()
            inverse_roots(2)
            for t in range(NT):
                dve.wait_ge(h2_turned, t + 1)
                V.tensor_copy(h2T[:, :, nodes(t)], turned_features(6 + t % 2, 0, rows(t))).then_inc(h2T_ready, 1)
            dve.wait_ge(hh_done, 2)
            for b in range(NB):
                last = V.tensor_copy(hhT[:, 1, bank_of(b)], ps[:, NB + b, 0:bank_len(b)])
            last.then_inc(hhT_ready, 1)

            dve.wait_ge(sup_ready, NT)
            V.tensor_copy(score[:, 0:FULL], support[:, 0:FULL, D])
            V.tensor_copy(score[:, FULL:NT], support[:, 0, D:D + 1])
            fence()
            V.tensor_copy(score[0:TAIL, FULL:NT], support[0:TAIL, FULL, D:D + 1])
            fence()
            V.reduce_max(nmx[:, :], score[:, :], axis=AX.X)
            V.drain().then_inc(score_max, 1)
            dve.wait_ge(score_turned, 1)
            V.tensor_reduce(nall[0:1, :], ps[0:1, 7, 0:P], AX.X, ALU.max, negate=True)
            V.drain().then_inc(score_top, 1)
            dve.wait_ge(score_spread, 1)
            V.tensor_copy(nall[:, :], ps[:, 7, 0:1])
            V.drain().then_inc(score_all, 1)
            dve.wait_ge(score_exp, 1)
            V.reduce_sum(ncol[:, :], natt[:, :], axis=AX.X)
            V.drain().then_inc(score_sum, 1)
            dve.wait_ge(score_tot, 1)
            V.reciprocal(ntot[:, :], ps[:, 7, 0:1])
            fence()
            V.tensor_scalar(natt[:, :], natt[:, :], ntot[:, 0:1], None, ALU.mult)
            V.drain().then_inc(natt_ready, 1)

            for t in range(NT + 3):
                if t < NT:
                    r, b = rows(t), t % 2
                    dve.wait_ge(e_done, t + 1)
                    dve.wait_ge(negm_ready, t + 1)
                    if t >= 2:
                        dve.wait_ge(pa_turned, NB * (t - 1))
                    V.tensor_tensor_reduce(out=em[0:r, b, :], in0=logits_of(0)[0:r, :], in1=negm[0:r, b, :],
                                           scale=1.0, scalar=-3.0e38, op0=ALU.add, op1=ALU.max,
                                           accum_out=edge_max[0:r, t:t + 1])
                    fence()
                    V.tensor_scalar(nm1[0:r, t:t + 1], edge_max[0:r, t:t + 1], -1.0, None, ALU.mult)
                    V.drain().then_inc(em_ready, 1)
                if t >= 3:
                    u = t - 3
                    r, b = rows(u), u % 2
                    dve.wait_ge(out_sum, u + 1)
                    dve.wait_ge(xb_ready, u + 1)
                    V.scalar_tensor_tensor(Z[0:r, u, :], ps[0:r, 6 + b, 0:D], final[0:r, u:u + 1], Z[0:r, u, :],
                                           ALU.mult, ALU.add).then_inc(out_ready, 1)
                if t < NT:
                    r, b = rows(t), t % 2
                    dve.wait_ge(p_ready, t + 1)
                    V.tensor_tensor(em[0:r, b, :], em[0:r, b, :], adj_n[0:r, t, :], ALU.mult).then_inc(pa_ready, 1)
                    V.reciprocal(t0[0:r, t:t + 1], edge_sum[0:r, t:t + 1])
                    fence()
                    V.tensor_tensor(final[0:r, t:t + 1], t0[0:r, t:t + 1], natt[0:r, t:t + 1], ALU.mult)

        @block.tensor
        def _(pe):
            T = nc.tensor

            def turn(dst, src, r):
                return T.transpose(dst, src, ident[0:r, 0:r])

            def turn_features(src, ready, free, done):
                for t in range(NT):
                    r, b = rows(t), t % 2
                    pe.wait_ge(ready, t + 1)
                    if t >= 2:
                        pe.wait_ge(free, t - 1)
                    for c in range(DC):
                        last = turn(ps[:, 6 + b, c * P:c * P + r], src[0:r, t, c * P:(c + 1) * P], r)
                    last.then_inc(done, 1)

            def projections(s, XT):
                for base, W in ((0, W1s), (NB, W3s)):
                    for b in range(NB):
                        for c in range(DC):
                            last = T.matmul(ps[0:H, base + b, 0:bank_len(b)], W[:, c, :], XT[:, c, bank_of(b)],
                                            start=(c == 0), stop=(c == DC - 1))
                    last.then_inc(qk_done, 1)
                pe.wait_ge(q_copied, s + 1)
                for b in range(NB):
                    last = T.matmul(ps[0:H, b, 0:bank_len(b)], W2s[:, :], QT[:, bank_of(b)], start=True, stop=True)
                last.then_inc(qk_done, 1)

            def logits(s):
                pe.wait_ge(q2_copied, s + 1)
                pe.wait_ge(k_copied, s + 1)
                for t in range(NT):
                    r = rows(t)
                    if t >= 2:
                        pe.wait_ge(exp_done, s * NT + t - 1)
                    for b in range(NB):
                        last = T.matmul(ps[0:r, 3 * (t % 2) + b, 0:bank_len(b)], Q2T[:, nodes(t)], KT[:, bank_of(b)],
                                        start=True, stop=True)
                    last.then_inc(logits_done, 1)

            def sx():
                pe.wait_ge(st_diag, NT)
                for t in range(NT):
                    r, b = rows(t), t % 2
                    if t >= 2:
                        pe.wait_ge(sx_ready, t - 1)
                    for k in range(NT):
                        q = rows(k)
                        last = T.matmul(ps[0:r, 6 + b, 0:D + 1], ST[0:q, k, nodes(t)], reg_h[0:q, k, :],
                                        start=(k == 0), stop=(k == NT - 1))
                    last.then_inc(sx_done, 1)

            def turn_g(t):
                r, b = rows(t), t % 2
                if t >= 2:
                    pe.wait_ge(gT_ready, t - 1)
                for c in range(DC):
                    last = turn(ps[:, 4 + b, c * P:c * P + r], FB[0:r, t, c * P:(c + 1) * P], r)
                last.then_inc(g_turned, 1)

            def gu(t):
                r, b = rows(t), t % 2
                pe.wait_ge(gT_ready, t + 1)
                if t >= 2:
                    pe.wait_ge(gu_ready, t - 1)
                for d in range(2):
                    for c in range(DC):
                        last = T.matmul(ps[0:r, 2 * b + d, :], GT[:, b, c * P:c * P + r],
                                        U12[:, d, c, :, :].rearrange("p s n -> p (s n)"),
                                        start=(c == 0), stop=(c == DC - 1))
                last.then_inc(gu_done, 1)

            def x3():
                for t in range(NT):
                    r, b = rows(t), t % 2
                    if t >= 2:
                        pe.wait_ge(x3_ready, t - 1)
                    for c in range(DC):
                        last = T.matmul(ps[0:r, 6 + b, :], XaT[:, c, nodes(t)],
                                        U3s[:, c, :, :].rearrange("p s n -> p (s n)"),
                                        start=(c == 0), stop=(c == DC - 1))
                    last.then_inc(x3_done, 1)

            def sv(t):
                r, b = rows(t), (NT + t) % 2
                if t >= 2:
                    pe.wait_ge(sv_ready, t - 1)
                else:
                    pe.wait_ge(x3_ready, NT - 1 + t)
                for k in range(NT):
                    q = rows(k)
                    last = T.matmul(ps[0:r, 6 + b, :], ST[0:q, k, nodes(t)], FB[0:q, k, :],
                                    start=(k == 0), stop=(k == NT - 1))
                last.then_inc(sv_done, 1)

            def turn_blocks(base, src, r, done):
                for j in range(NT):
                    last = turn(ps[0:rows(j), base + j // TB, (j % TB) * P:(j % TB) * P + r], src[:, nodes(j)], r)
                    if j % TB == TB - 1 or j == NT - 1:
                        last.then_inc(done, 1)

            def weigh(t, n, rhs, ready, done):
                r, b = rows(t), t % 2
                for j in range(NT):
                    q = rows(j)
                    if j % TB == 0:
                        pe.wait_ge(ready, NB * n + j // TB + 1)
                    last = T.matmul(ps[0:r, 6 + b, 0:D], AT[0:q, b, j, 0:r], rhs[0:q, j, 0:D],
                                    start=(j == 0), stop=(j == NT - 1))
                last.then_inc(done, 1)

            def turn_xa(t):
                r, b = rows(t), t % 2
                pe.wait_ge(xa_ready, t + 1)
                for c in range(DC):
                    last = turn(ps[:, 6 + b, D + c * P:D + c * P + r], xa[0:r, b, c * P:(c + 1) * P], r)
                last.then_inc(xa_turned, 1)

            def attend(s):
                for t in range(NT):
                    g = s * NT + t
                    pe.wait_ge(A_ready, g + 1)
                    if t >= 2:
                        pe.wait_ge(AT_ready, NB * (g - 1))
                    turn_blocks(3 * (t % 2), E[0:rows(t), t, :], rows(t), A_turned)
                    if s == 0 and t >= 1:
                        turn_xa(t - 1)
                    if t >= 2:
                        if s == 0:
                            pe.wait_ge(xaT_ready, t - 1)
                        else:
                            pe.wait_ge(y_ready, t - 1)
                    weigh(t, g, h, AT_ready, ax_done)
                if s == 0:
                    turn_xa(NT - 1)

            def turn_needs(s):
                pe.wait_ge(need_ready, s + 1)
                turn(ps[0:NT, 6 if s == 0 else 0, 0:P], need[:, :], P).then_inc(need_turned, 1)

            pe.wait_ge(const_ready, 3)
            turn_features(h, h_ready, hT_ready, h_turned)
            pe.wait_ge(hT_ready, NT)
            pe.wait_ge(w_in, 16 * 3)
            projections(0, hT)
            logits(0)
            sx()
            pe.wait_ge(exp_done, NT)
            pe.wait_ge(u_in, 16 * 6)
            pe.wait_ge(inv_ready, 1)
            turn_g(0)
            for t in range(NT):
                if t + 1 < NT:
                    turn_g(t + 1)
                gu(t)
                if t == NT - 4:
                    turn_needs(0)
            pe.wait_ge(gu_ready, NT)
            attend(0)
            pe.wait_ge(xaT_ready, NT)
            projections(1, XaT)
            logits(1)
            x3()
            for t in range(NT):
                sv(t)
                if t == NT - 4:
                    pe.wait_ge(exp_done, 2 * NT)
                    turn_needs(1)
            pe.wait_ge(sv_ready, NT)
            attend(1)

            turn_features(h, h2_ready, h2T_ready, h2_turned)
            pe.wait_ge(h2T_ready, NT)
            for m in range(DC):
                for b in range(NB):
                    for c in range(DC):
                        last = T.matmul(ps[:, NB * m + b, 0:bank_len(b)], EW[:, c, m * P:(m + 1) * P],
                                        h2T[:, c, bank_of(b)], start=(c == 0), stop=(c == DC - 1))
                last.then_inc(hh_done, 1)
            for t in range(NT):
                r, b = rows(t), t % 2
                if t >= 2:
                    pe.wait_ge(sup_ready, t - 1)
                for c in range(DC):
                    last = T.matmul(ps[0:r, 6 + b, 0:D + 1], h2T[:, c, nodes(t)], WN[:, c, :],
                                    start=(c == 0), stop=(c == DC - 1))
                last.then_inc(sup_done, 1)

            def edges(t):
                r = rows(t)
                if t >= 1:
                    pe.wait_ge(em_ready, t)
                for b in range(NB):
                    for c in range(DC):
                        last = T.matmul(ps[0:r, b, 0:bank_len(b)], hhT[:, c, nodes(t)], hhT[:, c, bank_of(b)],
                                        start=(c == 0), stop=(c == DC - 1))
                last.then_inc(e_done, 1)

            pe.wait_ge(hhT_ready, DC)
            edges(0)
            pe.wait_ge(score_max, 1)
            turn(ps[0:1, 7, 0:P], nmx[:, :], P).then_inc(score_turned, 1)
            pe.wait_ge(score_top, 1)
            T.matmul(ps[:, 7, 0:1], ones_row, nall[0:1, :], start=True, stop=True).then_inc(score_spread, 1)
            pe.wait_ge(score_sum, 1)
            T.matmul(ps[:, 7, 0:1], ones_all[:, :], ncol[:, :], start=True, stop=True).then_inc(score_tot, 1)
            for t in range(NT + 1):
                if t + 1 < NT:
                    edges(t + 1)
                if t < NT:
                    pe.wait_ge(pa_ready, t + 1)
                    if t >= 1:
                        pe.wait_ge(paT_ready, NB * t)
                    turn_blocks(3, em[0:rows(t), t % 2, :], rows(t), pa_turned)
                if t >= 1:
                    u = t - 1
                    if u == 1:
                        pe.wait_ge(natt_ready, 1)
                    if u >= 2:
                        pe.wait_ge(out_ready, u - 1)
                    weigh(u, u, support, paT_ready, out_sum)


_INS = ['x', 'adj', 'adj_t', 'L0_gnn_W1', 'L0_gnn_W2', 'L0_gnn_W3', 'L0_gnn_U1', 'L0_gnn_U2', 'L0_gnn_U3',
        'L0_gnn_gamma', 'L0_gnn_beta', 'L1_gnn_weight', 'L1_gnn_bias', 'L1_gnn_node_w', 'L1_gnn_edge_w']


def kernel(**inputs):
    import numpy as _np
    import concourse.bacc as _bacc
    from concourse import mybir as _mybir
    from concourse.bass_utils import run_bass_kernel_spmd as _run

    nc = _bacc.Bacc("TRN2", target_bir_lowering=False, num_devices=1)
    laid_out = dict(inputs, adj_t=_np.asarray(inputs['adj']).T)
    arrays, args = {}, []
    for name in _INS:
        a = _np.ascontiguousarray(laid_out[name])
        arrays[f"in_{name}_dram"] = a
        args.append(nc.dram_tensor(f"in_{name}_dram", a.shape, _mybir.dt.from_np(a.dtype), kind="ExternalInput").ap())
    y = nc.dram_tensor("out_0_dram", inputs['x'].shape, _mybir.dt.float32, kind="ExternalOutput").ap()
    gnn_block(nc, *args, y)
    r = _run(nc, [arrays], core_ids=[0])
    return r.results[0]["out_0_dram"]
```

```python
from contextlib import ExitStack

import concourse.bass as bass
from concourse import mybir

F32 = mybir.dt.float32
BF16 = mybir.dt.bfloat16
I32 = mybir.dt.int32
ALU = mybir.AluOpType
ACT = mybir.ActivationFunctionType
AX = mybir.AxisListType

P = 128
P_NUC = 0.9
LN_EPS = 1e-5
NEG_BIG = -9.0e15
HUGE = 1.0e30
HALVINGS = (6, 8)


def gnn_block(nc, x, adj, adj_t, W1, W2, W3, U1, U2, U3, gamma, beta, weight, bias, node_w, edge_w, out):
    N, D = x.shape
    H = W1.shape[1]
    NT = -(-N // P)
    FULL = N // P
    TAIL = N - FULL * P
    DC = D // P
    BANK = 512
    NB = -(-N // BANK)
    TB = BANK // P
    PAD = 8
    assert DC == 2 and N % 2 == 0 and NT == FULL + 1 and TAIL > 0 and NB == 3 and H <= P and 2 * D == BANK

    SHARED = 3
    OWN = NT - SHARED

    BY_POOL = NT - 2

    FIRST = range(0, (NB - 1) * TB)
    REST = range((NB - 1) * TB, NT)

    LOWEST = (1.0 - P_NUC) / N * 0.999
    MAX_ROUNDS = float(-(-N // 8))

    def rows(t):
        return P if t < FULL else TAIL

    def nodes(t):
        return slice(t * P, t * P + rows(t))

    def bank_of(b):
        return slice(b * BANK, min(N, (b + 1) * BANK))

    def bank_len(b):
        return min(N, (b + 1) * BANK) - b * BANK

    with ExitStack() as ctx:
        def sb(name, shape, dt=F32):
            return ctx.enter_context(nc.sbuf_tensor(name, shape, dt))

        def sem(name):
            return ctx.enter_context(nc.semaphore(name))

        reg_adj = sb("reg_adj", [P, NT, N])
        reg_rows = sb("reg_rows", [P, NT, N])
        reg_h = sb("reg_h", [P, NT, D + 1])
        reg_mix = sb("reg_mix", [P, NT * 2 * D])
        reg_t = sb("reg_t", [P, DC, N])
        reg_z = sb("reg_z", [P, NT * D])
        reg_at = sb("reg_at", [P, 2, NT * P])
        reg_u = sb("reg_u", [P, 2, DC, 2, D])
        below = sb("below", [P, N + PAD])

        ST = reg_adj
        E = reg_rows
        h = reg_h[:, :, 0:D]
        hT = reg_t
        XaT = reg_t
        Z = reg_z[:, :].rearrange("p (t d) -> p t d", t=NT)
        FB = reg_mix[:, :].rearrange("p (t d) -> p t d", t=NT)
        h2T = reg_mix[:, 0:DC * N].rearrange("p (c n) -> p c n", c=DC)
        hhT = reg_mix[:, NT * D:NT * D + DC * N].rearrange("p (c n) -> p c n", c=DC)
        AT = reg_at[:, :, :].rearrange("p b (j r) -> p b j r", j=NT)
        Q2T = reg_at[:, 0, 0:N]
        KT = reg_at[:, 1, 0:N]
        W1T = below[:, 0:DC * P]
        GT = reg_at[:, 0, 0:2 * D].rearrange("p (b d) -> p b d", b=2)
        share = reg_at[:, 1, 0:4 * D].rearrange("p (b d) -> p b d", b=2)
        unused = reg_at[:, 0, 2 * D:2 * D + N // 2].bitcast(BF16)
        other_below = reg_t[:, :, :].rearrange("p c n -> p (c n)")[:, DC * N - (N + PAD):DC * N]
        dropped = [half[:, i * N:(i + 1) * N] for half in (below[:, 0:N].bitcast(BF16), reg_t[:, 0, :].bitcast(BF16),
                                                           reg_t[:, 1, :].bitcast(BF16)) for i in range(2)]
        U12 = reg_u
        xa = reg_u[:, 0, 0, :, :]
        h2 = xa
        spare = reg_rows[:, 0:5, :].rearrange("p t n -> p (t n)")
        xres = spare[:, 0:NT * D].rearrange("p (t d) -> p t d", t=NT)
        o = NT * D
        gam, bet, bia = (spare[:, o + i * D:o + (i + 1) * D] for i in range(3))
        o += 3 * D
        EW = spare[:, o:o + DC * D].rearrange("p (c d) -> p c d", c=DC)
        o += DC * D
        WN = spare[:, o:o + DC * (D + 1)].rearrange("p (c d) -> p c d", c=DC)
        assert o + DC * (D + 1) <= 5 * N
        adj_n = reg_adj
        support = reg_h
        negm = reg_rows[:, 5:7, :]
        em = reg_rows[:, 7:9, :]

        W1s = sb("W1s", [P, DC, P])
        W3s = sb("W3s", [P, DC, P])
        W2s = sb("W2s", [P, P])
        U3s = sb("U3s", [P, DC, 2, D])
        ident = sb("ident", [P, P])
        ones_all = sb("ones_all", [P, P])
        ones_row = ones_all[0:1, :]

        (var, sd, rstd, t0, t1, nmr, nmax, tot, goal, mid, mass, reached, lo, hi, mass_hi, lo_c, hi_c, mass_c,
         need, kept, rkept, csum, inv_c, inv_r, nm1, edge_max, edge_sum, score, natt, final, span) = (
            sb(n, [P, NT]) for n in (
                "var", "sd", "rstd", "t0", "t1", "nmr", "nmax", "tot", "goal", "mid", "mass", "reached", "lo", "hi",
                "mass_hi", "lo_c", "hi_c", "mass_c", "need", "kept", "rkept", "csum", "inv_c", "inv_r", "nm1",
                "edge_max", "edge_sum", "score", "natt", "final", "span"))
        relu_sum, sign_sum, neg_mid = (sb(n, [P, SHARED]) for n in ("relu_sum", "sign_sum", "neg_mid"))
        nmx, nall, ncol, ntot = (sb(n, [P, 1]) for n in ("nmx", "nall", "ncol", "ntot"))
        stats = sb("stats", [P, NT, 6])
        mv = sb("mv", [P, NT, 2])
        factor = sb("factor", [P, max(HALVINGS), NT])
        rounds_f = sb("rounds_f", [NT, 1])
        rounds_i = sb("rounds_i", [NT, 1], I32)
        top = sb("top", [P, 8])
        taken = sb("taken", [P, 8])
        zero8 = sb("zero8", [P, 8])
        cum = sb("cum", [P, 9])

        ps = ctx.enter_context(nc.psum_tensor("ps", [P, 8, BANK], F32))

        x_in, w_in, u_in, st_in, sp_in, adj_in, out_done = (
            sem(n) for n in ("x_in", "w_in", "u_in", "st_in", "sp_in", "adj_in", "out_done"))
        st_diag, const_ready = sem("st_diag"), sem("const_ready")
        w_zero = sem("w_zero")
        var_ready, sd_ready, norm_ready = sem("var_ready"), sem("sd_ready"), sem("norm_ready")
        h_ready, h_turned, hT_ready = sem("h_ready"), sem("h_turned"), sem("hT_ready")
        w1_turned, w1T_ready, w12_done, w12_ready = (
            sem(n) for n in ("w1_turned", "w1T_ready", "w12_done", "w12_ready"))
        k_done, q2_done, k_copied, q2_copied = (sem(n) for n in ("k_done", "q2_done", "k_copied", "q2_copied"))
        logits_done, max_ready, exp_done = sem("logits_done"), sem("max_ready"), sem("exp_done")
        span_ready, factor_ready, mid_ready, shared_mass = (
            sem(n) for n in ("span_ready", "factor_ready", "mid_ready", "shared_mass"))
        sx_done, sx_ready, csum_done, inv_ready = sem("sx_done"), sem("sx_ready"), sem("csum_done"), sem("inv_ready")
        g_turned, gT_ready, gu_done, gu_ready = sem("g_turned"), sem("gT_ready"), sem("gu_done"), sem("gu_ready")
        x3_done, x3_ready, sv_done, sv_ready = sem("x3_done"), sem("x3_ready"), sem("sv_done"), sem("sv_ready")
        share_added = sem("share_added")
        need_ready, need_turned = sem("need_ready"), sem("need_turned")
        A_ready, A_turned, AT_ready, kept_ready = sem("A_ready"), sem("A_turned"), sem("AT_ready"), sem("kept_ready")
        below_ready = sem("below_ready")
        ax_done, xa_ready, xa_turned, xaT_ready = sem("ax_done"), sem("xa_ready"), sem("xa_turned"), sem("xaT_ready")
        y_ready = sem("y_ready")
        xbeta_ready, yn_ready, x1_ready, h2_ready, xb_ready = (
            sem(n) for n in ("xbeta_ready", "yn_ready", "x1_ready", "h2_ready", "xb_ready"))
        h2_turned, h2T_ready, hh_done, hhT_ready = sem("h2_turned"), sem("h2T_ready"), sem("hh_done"), sem("hhT_ready")
        sup_done, sup_ready = sem("sup_done"), sem("sup_ready")
        negm_ready, e_done, em_ready, p_ready, pa_ready = (
            sem(n) for n in ("negm_ready", "e_done", "em_ready", "p_ready", "pa_ready"))
        pa_turned, paT_ready, out_sum, out_ready = (
            sem(n) for n in ("pa_turned", "paT_ready", "out_sum", "out_ready"))
        score_max, score_turned, score_top, score_spread, score_all, score_exp, score_sum, score_tot, natt_ready = (
            sem(n) for n in ("score_max", "score_turned", "score_top", "score_spread", "score_all", "score_exp",
                             "score_sum", "score_tot", "natt_ready"))

        def logits_of(t):
            return ps[:, 3 * (t % 2):3 * (t % 2) + NB, :].rearrange("p b n -> p (b n)")[:, 0:N]

        def turned_features(bank, col, r):
            return ps[:, bank, col:col + D].rearrange("p (c r) -> p c r", c=DC)[:, :, 0:r]

        def below_of(s, t):
            return other_below if s == 1 and t % 2 == 1 else below

        def columns(tiles):
            return slice(tiles[0], tiles[-1] + 1)

        HH = ([(m, b) for b in range(NB - 1) for m in range(DC)], [(m, NB - 1) for m in range(DC)])
        HH_BANKS = (5, 3, 4, 5, 5, 3)

        def sup_bank(t):
            return (1 if t in FIRST else 6) + t % 2

        GU_SLOT = NT

        def bank_at(i):
            return (6 + i) % 8

        block = ctx.enter_context(nc.Block())

        @block.sync
        def _(sp):
            sp.dma_start(E[:, 0:FULL, 0:D], x[0:FULL * P, :].rearrange("(t p) d -> p t d", p=P)).then_inc(x_in, 16)
            sp.dma_start(E[0:TAIL, FULL, 0:D], x[FULL * P:N, :]).then_inc(x_in, 16)
            sp.dma_start(W1s[:, :, 0:H], W1.rearrange("(c p) n -> p c n", p=P)).then_inc(w_in, 16)
            sp.dma_start(W3s[:, :, 0:H], W3.rearrange("(c p) n -> p c n", p=P)).then_inc(w_in, 16)
            sp.wait_ge(w_zero, 1)
            sp.dma_start(W2s[0:H, 0:H], W2).then_inc(w_in, 16)
            for k in range(NT):
                sp.dma_start(ST[0:rows(k), k, :], adj_t[nodes(k), :]).then_inc(st_in, 16)
            for s in range(2):
                for dst, U in ((U12[:, 0, :, s, :], U1), (U12[:, 1, :, s, :], U2), (U3s[:, :, s, :], U3)):
                    sp.dma_start(dst, U[s, :, :].rearrange("(c p) n -> p c n", p=P)).then_inc(u_in, 16)
            sp.wait_ge(sv_done, NT)
            for t in range(NT):
                sp.dma_start(adj_n[0:rows(t), t, :], adj[nodes(t), :]).then_inc(adj_in, 16)
            sp.wait_ge(A_turned, NB * (NT + 5))
            sp.dma_start(xres[:, 0:FULL, :], x[0:FULL * P, :].rearrange("(t p) d -> p t d", p=P)).then_inc(sp_in, 16)
            sp.dma_start(xres[0:TAIL, FULL, :], x[FULL * P:N, :]).then_inc(sp_in, 16)
            for dst, src in ((gam, gamma), (bet, beta), (bia, bias)):
                sp.dma_start(dst, src.partition_broadcast(P)).then_inc(sp_in, 16)
            sp.dma_start(EW, edge_w.rearrange("(c p) n -> p c n", p=P)).then_inc(sp_in, 16)
            sp.dma_start(WN[:, :, 0:D], weight.rearrange("(c p) n -> p c n", p=P)).then_inc(sp_in, 16)
            with nc.allow_non_contiguous_dma(reason="node_w is one column of a few hundred values"):
                sp.dma_start(WN[:, :, D:D + 1], node_w.rearrange("(c p) n -> p c n", p=P)).then_inc(sp_in, 16)
            for t in range(NT):
                sp.wait_ge(out_ready, t + 1)
                sp.dma_start(out[nodes(t), :], Z[0:rows(t), t, :]).then_inc(out_done, 16)
            sp.wait_ge(out_done, 16 * NT)

        @block.gpsimd
        def _(pool):
            G = nc.gpsimd
            G.memset(W2s[:, :], 0.0).then_inc(w_zero, 1)
            if H < P:
                G.memset(W1s[:, :, H:P], 0.0)
                G.memset(W3s[:, :, H:P], 0.0)
            G.memset(ident[:, :], 0.0).then_inc(const_ready, 1)
            G.memset(ones_all[:, :], 1.0).then_inc(const_ready, 1)
            pool.wait_ge(const_ready, 2)
            G.affine_select(out=ident[:, :], in_=ident[:, :], compare_op=ALU.not_equal, fill=1.0, base=0,
                            pattern=[[-1, P]], channel_multiplier=1).then_inc(const_ready, 1)
            pool.wait_ge(const_ready, 3)
            for k in range(NT):
                r = rows(k)
                pool.wait_ge(st_in, 16 * NT)
                G.tensor_tensor(ST[0:r, k, nodes(k)], ST[0:r, k, nodes(k)], ident[0:r, 0:r],
                                ALU.add).then_inc(st_diag, 1)
            def add_share(i):
                stage, t = divmod(i, NT)
                r = rows(t)
                pool.wait_ge((gu_ready, x3_ready, sv_ready)[stage], t + 1)
                base = h if stage == 0 else Z
                G.tensor_tensor(Z[0:r, t, :], base[0:r, t, :], share[0:r, i % 2, 0:D], ALU.add)
                if stage != 1:
                    G.drain()
                    G.tensor_tensor(Z[0:r, t, :], Z[0:r, t, :], share[0:r, i % 2, D:2 * D], ALU.add)
                G.drain().then_inc(share_added, 1)

            def kept_part(t):
                r = rows(t)
                pool.wait_ge(below_ready, t + 1)
                G.tensor_tensor(E[0:r, t, :], E[0:r, t, :], below_of(1, t)[0:r, 0:N],
                                ALU.subtract).then_inc(A_ready, 1)

            def x_plus_beta(t):
                r = rows(t)
                G.tensor_tensor(xres[0:r, t, :], xres[0:r, t, :], bet[0:r, :], ALU.add).then_inc(xbeta_ready, 1)

            def absent(t):
                r = rows(t)
                if t >= 2:
                    pool.wait_ge(em_ready, t - 1)
                G.tensor_scalar(negm[0:r, t % 2, :], adj_n[0:r, t, :], 0.0, NEG_BIG,
                                ALU.is_le, ALU.mult).then_inc(negm_ready, 1)

            def first_outputs(tiles):
                for t in tiles:
                    r = rows(t)
                    pool.wait_ge(yn_ready, t + 1)
                    G.tensor_tensor(Z[0:r, t, :], Z[0:r, t, :], gam[0:r, :], ALU.mult)
                    G.drain()
                    pool.wait_ge(xbeta_ready, t + 1)
                    G.tensor_tensor(Z[0:r, t, :], Z[0:r, t, :], xres[0:r, t, :], ALU.add).then_inc(x1_ready, 1)

            for i in range(3 * NT):
                add_share(i)
            for t in range(BY_POOL):
                kept_part(t)
                if t == 6:
                    pool.wait_ge(sp_in, 16 * 8)
                    for u in range(NT):
                        x_plus_beta(u)
                if t == 7:
                    pool.wait_ge(adj_in, 16 * NT)
                    pool.wait_ge(A_turned, NB * (NT + 6))
                    absent(0)
            first_outputs(FIRST)
            pool.wait_ge(A_turned, NB * (NT + 7))
            absent(1)
            first_outputs(REST)
            for t in range(NT):
                r = rows(t)
                pool.wait_ge(h2_ready, t + 1)
                G.tensor_tensor(Z[0:r, t, :], Z[0:r, t, :], bia[0:r, :], ALU.add).then_inc(xb_ready, 1)
            for t in range(2, NT):
                absent(t)

        @block.scalar
        def _(act):
            A = nc.scalar

            def copy(dst, src):
                return A.activation(dst, src, ACT.Copy)

            def scaled(dst, src, by):
                return A.activation(dst, src, ACT.Copy, scale=by)

            def roots(n, tiles):
                act.wait_ge(var_ready, n + 1)
                A.activation(sd[:, columns(tiles)], var[:, columns(tiles)], ACT.Sqrt).then_inc(sd_ready, 1)

            def norms(n, tiles):
                roots(n, tiles)
                act.wait_ge(norm_ready, n + 1)
                for t in tiles:
                    r = rows(t)
                    A.activation(Z[0:r, t, :], Z[0:r, t, :], ACT.Identity, bias=nmr[0:r, t:t + 1],
                                 scale=rstd[0:r, t:t + 1]).then_inc(yn_ready, 1)

            def h2T_out(t):
                act.wait_ge(h2_turned, t + 1)
                copy(h2T[:, :, nodes(t)], turned_features(3 + t % 2, 0, rows(t))).then_inc(h2T_ready, 1)

            def second_norms(n, tiles):
                roots(n, tiles)
                act.wait_ge(norm_ready, n + 1)
                for t in tiles:
                    r = rows(t)
                    if t >= 2:
                        act.wait_ge(h2_turned, t - 1)
                    A.activation(h2[0:r, t % 2, :], Z[0:r, t, :], ACT.Relu, bias=nmr[0:r, t:t + 1],
                                 scale=rstd[0:r, t:t + 1]).then_inc(h2_ready, 1)
                    if t > tiles[0]:
                        h2T_out(t - 1)
                h2T_out(tiles[-1])

            def hh_out(group):
                first = len(HH[0]) * group
                for i, (m, b) in enumerate(HH[group], start=first):
                    act.wait_ge(hh_done, i + 1)
                    copy(hhT[:, m, bank_of(b)], ps[:, HH_BANKS[i], 0:bank_len(b)]).then_inc(hhT_ready, 1)

            def sup_out(tiles):
                for t in tiles:
                    r = rows(t)
                    act.wait_ge(sup_done, t + 1)
                    copy(support[0:r, t, :], ps[0:r, sup_bank(t), 0:D + 1]).then_inc(sup_ready, 1)

            def queries(s):
                for b in range(NB):
                    act.wait_ge(q2_done, NB * s + b + 1)
                    copy(Q2T[:, bank_of(b)], ps[:, b, 0:bank_len(b)]).then_inc(q2_copied, 1)

            def exps(s):
                for t in range(NT):
                    r = rows(t)
                    act.wait_ge(max_ready, s * NT + t + 1)
                    A.activation(E[0:r, t, :], logits_of(t)[0:r, :], ACT.Exp, bias=nmax[0:r, t:t + 1],
                                 accum_out=tot[0:r, t:t + 1]).then_inc(exp_done, 1)
                act.wait_ge(span_ready, s + 1)
                for k in range(HALVINGS[s]):
                    A.activation(factor[:, k, :], factor[:, k - 1, :] if k else span[:, :], ACT.Sqrt)
                    A.drain().then_inc(factor_ready, 1)

            def shared_masses(s, k):
                act.wait_ge(mid_ready, sum(HALVINGS[:s]) + k + 1)
                for q in range(SHARED):
                    t = OWN + q
                    r = rows(t)
                    for func, dst in ((ACT.Relu, relu_sum), (ACT.Sign, sign_sum)):
                        A.activation(unused[0:r, :], E[0:r, t, :], func, bias=neg_mid[0:r, q:q + 1],
                                     accum_out=dst[0:r, q:q + 1])
                        A.drain()
                    if q == SHARED - 1:
                        A.drain().then_inc(shared_mass, 1)
                    between(s, k * SHARED + q)

            def column_sum(k):
                r = rows(k)
                A.activation(unused[0:r, :], ST[0:r, k, :], ACT.Copy, accum_out=csum[0:r, k:k + 1])
                A.drain().then_inc(csum_done, 1)

            def sx_out(t):
                r = rows(t)
                act.wait_ge(sx_done, t + 1)
                copy(FB[0:r, t, 0:D + 1], ps[0:r, bank_at(t), 0:D + 1]).then_inc(sx_ready, 1)

            def share_buffer(i):
                if i >= 2:
                    act.wait_ge(share_added, i - 1)
                return share[:, i % 2, :]

            def gt_out(t):
                act.wait_ge(g_turned, t + 1)
                if t >= 2:
                    act.wait_ge(gu_done, t - 1)
                copy(GT[:, t % 2, :], ps[:, 4 + t % 2, 0:D]).then_inc(gT_ready, 1)

            def gu_out(t):
                r, b = rows(t), t % 2
                act.wait_ge(gu_done, t + 1)
                dst = share_buffer(t)
                for d, inv in enumerate((inv_r, inv_c)):
                    src, by = ps[0:r, 2 * b + d, :], inv[0:r, t:t + 1]
                    scaled(dst[0:r, d * D:(d + 1) * D], src[:, 0:D], by)
                    last = scaled(FB[0:r, t, d * D:(d + 1) * D], src[:, D:2 * D], by)
                last.then_inc(gu_ready, 1)

            def g_out(t):
                if t + 1 < NT:
                    gt_out(t + 1)
                if t == 0:
                    act.wait_ge(inv_ready, 1)
                gu_out(t)

            def x3_out(t):
                r = rows(t)
                act.wait_ge(x3_done, t + 1)
                dst = share_buffer(NT + t)
                copy(dst[0:r, 0:D], ps[0:r, bank_at(t), 0:D])
                copy(h[0:r, t, :], ps[0:r, bank_at(t), D:2 * D]).then_inc(x3_ready, 1)

            def sv_out(t):
                r, b = rows(t), bank_at(NT + t)
                act.wait_ge(sv_done, t + 1)
                dst = share_buffer(2 * NT + t)
                scaled(dst[0:r, 0:D], ps[0:r, b, 0:D], inv_r[0:r, t:t + 1])
                scaled(dst[0:r, D:2 * D], ps[0:r, b, D:2 * D], inv_c[0:r, t:t + 1]).then_inc(sv_ready, 1)

            SV_SLOTS = tuple(6 + 2 * t for t in range(NT))

            def between(s, slot):
                if s == 0:
                    if slot < NT:
                        sx_out(slot)
                        column_sum(slot)
                    if slot == NT - 1:
                        gt_out(0)
                    if GU_SLOT <= slot:
                        g_out(slot - GU_SLOT)
                else:
                    for t in range(NT * slot // SV_SLOTS[0], min(NT, NT * (slot + 1) // SV_SLOTS[0])):
                        x3_out(t)
                    if slot in SV_SLOTS:
                        sv_out(SV_SLOTS.index(slot))

            def rows_out(base, b, r, turned, ready, n):
                for k in range(NB):
                    act.wait_ge(turned, NB * n + k + 1)
                    j0, j1 = k * TB, min(FULL, (k + 1) * TB)
                    src = ps[:, base + k, :].rearrange("p (j r) -> p j r", j=TB)
                    last = copy(AT[:, b, j0:j1, 0:r], src[:, 0:j1 - j0, 0:r])
                    if k == NB - 1:
                        last = copy(AT[0:TAIL, b, FULL, 0:r], src[0:TAIL, FULL - j0, 0:r])
                    last.then_inc(ready, 1)

            def attend(s):
                act.wait_ge(share_added, NT if s == 0 else 3 * NT)
                for t in range(NT):
                    g = s * NT + t
                    r, b = rows(t), t % 2
                    if g >= 2:
                        act.wait_ge(ax_done, g - 1)
                    rows_out(0, b, r, A_turned, AT_ready, g)
                    if s == 0:
                        if t >= 1:
                            xaT_out(t - 1)
                        act.wait_ge(ax_done, t + 1)
                        act.wait_ge(kept_ready, t + 1)
                        scaled(xa[0:r, b, :], ps[0:r, 6 + b, 0:D], rkept[0:r, t:t + 1]).then_inc(xa_ready, 1)
                    elif t == NT - 3:
                        norms(1, FIRST)
                    elif t == NT - 2:
                        second_norms(2, FIRST)
                        hh_out(0)
                if s == 0:
                    xaT_out(NT - 1)

            def xaT_out(t):
                act.wait_ge(xa_turned, t + 1)
                copy(XaT[:, :, nodes(t)], turned_features(6 + t % 2, D, rows(t))).then_inc(xaT_ready, 1)

            act.wait_ge(w1_turned, 1)
            copy(W1T, ps[:, 0, 0:DC * P]).then_inc(w1T_ready, 1)
            act.wait_ge(w12_done, 1)
            copy(W1s[:, :, :].rearrange("p c n -> p (c n)"), ps[:, 1, 0:DC * P]).then_inc(w12_ready, 1)

            roots(0, range(NT))
            act.wait_ge(norm_ready, 1)
            for t in range(NT):
                r = rows(t)
                A.activation(h[0:r, t, :], E[0:r, t, 0:D], ACT.Relu, bias=nmr[0:r, t:t + 1],
                             scale=rstd[0:r, t:t + 1]).then_inc(h_ready, 1)

            for s in range(2):
                queries(s)
                exps(s)
                if s == 0:
                    act.wait_ge(st_diag, NT)
                for k in range(HALVINGS[s]):
                    shared_masses(s, k)
                slots = HALVINGS[s] * SHARED
                if s == 0:
                    for t in range(slots - GU_SLOT, NT):
                        g_out(t)
                else:
                    for t in range(NT):
                        if SV_SLOTS[t] >= slots:
                            sv_out(t)
                attend(s)

            sup_out(FIRST[0:3])
            norms(3, REST)
            sup_out(FIRST[3:])
            second_norms(4, REST)
            hh_out(1)

            def edge_exp(t):
                r, b = rows(t), t % 2
                act.wait_ge(em_ready, t + 1)
                A.activation(em[0:r, b, :], em[0:r, b, :], ACT.Exp, bias=nm1[0:r, t:t + 1],
                             accum_out=edge_sum[0:r, t:t + 1]).then_inc(p_ready, 1)

            sup_out(REST[0:2])
            edge_exp(0)
            sup_out(REST[2:])
            act.wait_ge(score_all, 1)
            A.activation(natt[:, 0:FULL], support[:, 0:FULL, D], ACT.Exp, bias=nall[:, :])
            A.activation(natt[0:TAIL, FULL:NT], support[0:TAIL, FULL, D:D + 1], ACT.Exp,
                         bias=nall[0:TAIL, :]).then_inc(score_exp, 1)
            for t in range(1, NT + 1):
                if t < NT:
                    edge_exp(t)
                u = t - 1
                if u >= 2:
                    act.wait_ge(out_sum, u - 1)
                rows_out(3, u % 2, rows(u), pa_turned, paT_ready, u)

        @block.vector
        def _(dve):
            V = nc.vector

            def fence():
                V.drain()

            def variances(tiles):
                fence()
                for t in tiles:
                    V.bn_aggr(mv[0:rows(t), t, :], stats[0:rows(t), t, :])
                fence()
                V.tensor_scalar(var[:, columns(tiles)], mv[:, columns(tiles), 1], LN_EPS, None, ALU.add)
                V.drain().then_inc(var_ready, 1)

            def inverse_roots(n, tiles):
                c = columns(tiles)
                dve.wait_ge(sd_ready, n + 1)
                V.reciprocal(rstd[:, c], sd[:, c])
                fence()
                V.tensor_tensor(t0[:, c], rstd[:, c], rstd[:, c], ALU.mult)
                fence()
                V.tensor_tensor(t0[:, c], t0[:, c], var[:, c], ALU.mult)
                fence()
                V.tensor_scalar(t0[:, c], t0[:, c], -0.5, 1.5, ALU.mult, ALU.add)
                fence()
                V.tensor_tensor(rstd[:, c], rstd[:, c], t0[:, c], ALU.mult)
                fence()
                V.scalar_tensor_tensor(nmr[:, c], mv[:, c, 0], -1.0, rstd[:, c], ALU.mult, ALU.mult)
                V.drain().then_inc(norm_ready, 1)

            def x1_statistics(tiles):
                for t in tiles:
                    dve.wait_ge(x1_ready, t + 1)
                    V.bn_stats(stats[0:rows(t), t, :], Z[0:rows(t), t, :])
                variances(tiles)

            def keys(s):
                dve.wait_ge(k_done, NB * (s + 1))
                for b in range(NB):
                    last = V.tensor_copy(KT[:, bank_of(b)], ps[:, NB + b, 0:bank_len(b)])
                last.then_inc(k_copied, 1)

            def maxima(s):
                for t in range(NT):
                    r = rows(t)
                    dve.wait_ge(logits_done, s * NT + t + 1)
                    V.tensor_reduce(nmax[0:r, t:t + 1], logits_of(t)[0:r, :], AX.X, ALU.max, negate=True)
                    V.drain().then_inc(max_ready, 1)

            def middle(s, k):
                dve.wait_ge(factor_ready, sum(HALVINGS[:s]) + k + 1)
                V.tensor_tensor(mid[:, :], lo[:, :], factor[:, k, :], ALU.mult)
                V.scalar_tensor_tensor(neg_mid[:, :], lo[:, OWN:NT], -1.0, factor[:, k, OWN:NT], ALU.mult, ALU.mult)
                V.drain().then_inc(mid_ready, 1)

            def halve(s, k):
                if s == 1 and k == 1:
                    dve.wait_ge(x3_done, NT)
                buffers = 2 if s == 1 and k == 0 else len(dropped)
                for t in range(OWN):
                    V.scalar_tensor_tensor(dropped[t % buffers], E[:, t, :], mid[:, t:t + 1], E[:, t, :],
                                           ALU.is_ge, ALU.mult, accum_out=mass[:, t:t + 1])
                    if t % buffers == buffers - 1:
                        fence()
                fence()
                if s == 0 and k == NT // SHARED:
                    inverse_sums()
                dve.wait_ge(shared_mass, sum(HALVINGS[:s]) + k + 1)
                V.scalar_tensor_tensor(t0[:, 0:SHARED], sign_sum[:, :], float(N), mid[:, OWN:NT],
                                       ALU.add, ALU.mult)
                fence()
                V.scalar_tensor_tensor(mass[:, OWN:NT], t0[:, 0:SHARED], 0.5, relu_sum[:, :], ALU.mult, ALU.add)
                fence()
                V.tensor_tensor(reached[:, :], mass[:, :], goal[:, :], ALU.is_ge)
                fence()
                V.tensor_tensor(lo_c[:, :], mid[:, :], reached[:, :], ALU.mult)
                V.scalar_tensor_tensor(hi_c[:, :], reached[:, :], HUGE, mid[:, :], ALU.mult, ALU.add)
                V.scalar_tensor_tensor(mass_c[:, :], reached[:, :], -HUGE, mass[:, :], ALU.mult, ALU.add)
                fence()
                V.tensor_tensor(lo[:, :], lo[:, :], lo_c[:, :], ALU.max)
                V.tensor_tensor(hi[:, :], hi[:, :], hi_c[:, :], ALU.min)
                V.tensor_tensor(mass_hi[:, :], mass_hi[:, :], mass_c[:, :], ALU.max)
                fence()
                if k + 1 < HALVINGS[s]:
                    middle(s, k + 1)

            def bracket(s):
                dve.wait_ge(exp_done, NT * (s + 1))
                V.tensor_scalar(lo[:, :], tot[:, :], LOWEST, None, ALU.mult)
                fence()
                V.reciprocal(span[:, :], lo[:, :])
                V.drain().then_inc(span_ready, 1)
                V.tensor_scalar(goal[:, :], tot[:, :], P_NUC, None, ALU.mult)
                V.memset(hi[:, :], 2.0)
                V.memset(mass_hi[:, :], 0.0)
                fence()
                middle(s, 0)
                for k in range(HALVINGS[s]):
                    halve(s, k)
                for t in range(OWN, NT):
                    r = rows(t)
                    V.scalar_tensor_tensor(dropped[t - OWN][0:r, :], E[0:r, t, :], hi[0:r, t:t + 1], E[0:r, t, :],
                                           ALU.is_gt, ALU.mult, accum_out=mass_hi[0:r, t:t + 1])
                fence()

            def inverse_sums():
                dve.wait_ge(csum_done, NT)
                dve.wait_ge(sx_ready, NT)
                V.tensor_scalar(t1[:, :], csum[:, :], 1e-12, None, ALU.max)
                V.tensor_scalar(t0[:, 0:FULL], FB[:, 0:FULL, D], 1e-12, None, ALU.max)
                V.tensor_scalar(t0[0:TAIL, FULL:NT], FB[0:TAIL, FULL, D:D + 1], 1e-12, None, ALU.max)
                fence()
                V.reciprocal(inv_c[:, :], t1[:, :])
                V.reciprocal(inv_r[:, 0:FULL], t0[:, 0:FULL])
                V.reciprocal(inv_r[0:TAIL, FULL:NT], t0[0:TAIL, FULL:NT])
                V.drain().then_inc(inv_ready, 1)

            def round_counts(s):
                V.reciprocal(t0[:, :], lo[:, :])
                V.tensor_tensor(t1[:, :], goal[:, :], mass_hi[:, :], ALU.subtract)
                fence()
                V.tensor_tensor(t0[:, :], t0[:, :], t1[:, :], ALU.mult)
                fence()
                for sl, q in ((slice(0, P), slice(0, FULL)), (slice(0, TAIL), slice(FULL, NT))):
                    V.tensor_scalar(need[sl, q], t0[sl, q], 1.0 / 8, 0.501, ALU.mult, ALU.add)
                V.drain().then_inc(need_ready, 1)
                dve.wait_ge(need_turned, s + 1)
                V.reduce_max(rounds_f[:, :], ps[0:NT, 6 if s == 0 else 1, 0:P], axis=AX.X)
                fence()
                V.tensor_scalar(rounds_f[:, :], rounds_f[:, :], MAX_ROUNDS, 1.0, ALU.min, ALU.max)
                fence()
                V.tensor_scalar(rounds_f[:, :], rounds_f[:, :], 2.0 ** 23, None, ALU.add)
                fence()
                V.tensor_scalar(rounds_f[:, :], rounds_f[:, :], 2.0 ** 23, None, ALU.subtract)
                fence()
                V.tensor_copy(rounds_i[:, :], rounds_f[:, :])
                fence()

            def take(s, count):
                if s == 1:
                    V.memset(other_below[:, N:N + PAD], 0.0)
                for t in range(NT):
                    r = rows(t)
                    left = below_of(s, t)
                    if s == 1 and t >= 2:
                        dve.wait_ge(A_ready, NT + t - 1)
                    V.scalar_tensor_tensor(left[0:r, 0:N], E[0:r, t, :], hi[0:r, t:t + 1], E[0:r, t, :],
                                           ALU.is_lt if t < OWN else ALU.is_le, ALU.mult)
                    V.tensor_copy(cum[0:r, 8:9], mass_hi[0:r, t:t + 1])
                    if s == 1 and t == NT - 2:
                        inverse_roots(1, FIRST)
                    if s == 1 and t == NT - 1:
                        x1_statistics(FIRST)
                        inverse_roots(2, FIRST)
                    V.reg_load(count, rounds_i[t:t + 1, 0:1])
                    fence()
                    with V.Fori(0, count):
                        V.max(out=top[0:r, :], in_=left[0:r, :])
                        V.tensor_copy(cum[0:r, 0:1], cum[0:r, 8:9])
                        fence()
                        V.tensor_tensor_scan(cum[0:r, 1:9], top[0:r, :], zero8[0:r, :], cum[0:r, 0:1],
                                             ALU.add, ALU.add)
                        fence()
                        V.scalar_tensor_tensor(taken[0:r, :], cum[0:r, 0:8], goal[0:r, t:t + 1], top[0:r, :],
                                               ALU.is_lt, ALU.mult)
                        fence()
                        V.match_replace(out=left[0:r, :], in_to_replace=taken[0:r, :], in_values=left[0:r, :],
                                        imm_value=0.0)
                        fence()
                    if s == 1 and t < BY_POOL:
                        V.drain().then_inc(below_ready, 1)
                    else:
                        if s == 1:
                            dve.wait_ge(A_ready, NT + BY_POOL)
                        V.scalar_tensor_tensor(E[0:r, t, :], left[0:r, 0:N], -1.0, E[0:r, t, :], ALU.mult, ALU.add,
                                               accum_out=kept[0:r, t:t + 1])
                        V.drain().then_inc(A_ready, 1)
                    if s == 0:
                        V.reciprocal(rkept[0:r, t:t + 1], kept[0:r, t:t + 1]).then_inc(kept_ready, 1)
                    if s == 1 and 2 <= t <= NT - 3:
                        sum_up(t - 2)
                    if s == 1 and t >= NT - 3:
                        sum_up(t - 1)
                    if s == 1 and t == NT - 3:
                        assert t - 1 == FIRST[-1]
                        variances(FIRST)

            def sum_up(t):
                r, b = rows(t), t % 2
                dve.wait_ge(share_added, 2 * NT + t + 1)
                dve.wait_ge(ax_done, NT + t + 1)
                V.reciprocal(rkept[0:r, t:t + 1], ps[0:r, 6 + b, D:D + 1])
                fence()
                V.scalar_tensor_tensor(Z[0:r, t, :], ps[0:r, 6 + b, 0:D], rkept[0:r, t:t + 1], Z[0:r, t, :],
                                       ALU.mult, ALU.add).then_inc(y_ready, 1)
                fence()
                V.bn_stats(stats[0:r, t, :], Z[0:r, t, :])

            for table, value in ((zero8, 0.0), (tot, 1.0), (mass, 0.0), (need, 0.0), (csum, 1.0), (score, 0.0),
                                 (natt, 0.0), (relu_sum, 0.0), (sign_sum, 0.0)):
                V.memset(table[:, :], value)
            V.memset(mv[:, :, :], 1.0)
            V.memset(below[:, N:N + PAD], 0.0)
            V.memset(reg_h[:, :, D:D + 1], 1.0)
            fence()

            dve.wait_ge(x_in, 32)
            for t in range(NT):
                V.bn_stats(stats[0:rows(t), t, :], E[0:rows(t), t, 0:D])
            variances(range(NT))
            inverse_roots(0, range(NT))
            for t in range(NT):
                dve.wait_ge(h_turned, t + 1)
                V.tensor_copy(hT[:, :, nodes(t)], turned_features(6 + t % 2, 0, rows(t))).then_inc(hT_ready, 1)

            count = V.alloc_register("rounds")
            for s in range(2):
                keys(s)
                maxima(s)
                bracket(s)
                round_counts(s)
                take(s, count)

            sum_up(NT - 1)
            variances(REST)
            inverse_roots(3, REST)
            x1_statistics(REST)
            inverse_roots(4, REST)

            def masked(t):
                r, b = rows(t), t % 2
                dve.wait_ge(e_done, t + 1)
                dve.wait_ge(negm_ready, t + 1)
                if t >= 2:
                    dve.wait_ge(pa_turned, NB * (t - 1))
                V.tensor_tensor_reduce(out=em[0:r, b, :], in0=logits_of(0)[0:r, :], in1=negm[0:r, b, :],
                                       scale=1.0, scalar=-3.0e38, op0=ALU.add, op1=ALU.max,
                                       accum_out=edge_max[0:r, t:t + 1])
                fence()
                V.tensor_scalar(nm1[0:r, t:t + 1], edge_max[0:r, t:t + 1], -1.0, None, ALU.mult)
                V.drain().then_inc(em_ready, 1)

            def weighted(t):
                r, b = rows(t), t % 2
                dve.wait_ge(p_ready, t + 1)
                V.tensor_tensor(em[0:r, b, :], em[0:r, b, :], adj_n[0:r, t, :], ALU.mult).then_inc(pa_ready, 1)

            def factors(t):
                r = rows(t)
                V.reciprocal(t0[0:r, t:t + 1], edge_sum[0:r, t:t + 1])
                fence()
                V.tensor_tensor(final[0:r, t:t + 1], t0[0:r, t:t + 1], natt[0:r, t:t + 1], ALU.mult)

            def output(t):
                r = rows(t)
                dve.wait_ge(out_sum, t + 1)
                dve.wait_ge(xb_ready, t + 1)
                V.scalar_tensor_tensor(Z[0:r, t, :], ps[0:r, 6 + t % 2, 0:D], final[0:r, t:t + 1], Z[0:r, t, :],
                                       ALU.mult, ALU.add).then_inc(out_ready, 1)

            masked(0)
            weighted(0)

            dve.wait_ge(sup_ready, NT)
            V.tensor_copy(score[:, 0:FULL], support[:, 0:FULL, D])
            V.tensor_copy(score[:, FULL:NT], support[:, 0, D:D + 1])
            fence()
            V.tensor_copy(score[0:TAIL, FULL:NT], support[0:TAIL, FULL, D:D + 1])
            fence()
            V.reduce_max(nmx[:, :], score[:, :], axis=AX.X)
            V.drain().then_inc(score_max, 1)
            dve.wait_ge(score_turned, 1)
            V.tensor_reduce(nall[0:1, :], ps[0:1, 7, 0:P], AX.X, ALU.max, negate=True)
            V.drain().then_inc(score_top, 1)
            dve.wait_ge(score_spread, 1)
            V.tensor_copy(nall[:, :], ps[:, 7, 0:1])
            V.drain().then_inc(score_all, 1)
            dve.wait_ge(score_exp, 1)
            V.reduce_sum(ncol[:, :], natt[:, :], axis=AX.X)
            V.drain().then_inc(score_sum, 1)
            dve.wait_ge(score_tot, 1)
            V.reciprocal(ntot[:, :], ps[:, 7, 0:1])
            fence()
            V.tensor_scalar(natt[:, :], natt[:, :], ntot[:, 0:1], None, ALU.mult)
            V.drain().then_inc(natt_ready, 1)

            fence()
            factors(0)
            for t in range(1, NT + 3):
                if t < NT:
                    masked(t)
                if t >= 3:
                    output(t - 3)
                if t < NT:
                    weighted(t)
                    factors(t)

        @block.tensor
        def _(pe):
            T = nc.tensor

            def turn(dst, src, r):
                return T.transpose(dst, src, ident[0:r, 0:r])

            def weights():
                for c in range(DC):
                    last = turn(ps[:, 0, c * P:(c + 1) * P], W1s[:, c, :], P)
                last.then_inc(w1_turned, 1)
                pe.wait_ge(w1T_ready, 1)
                for c in range(DC):
                    last = T.matmul(ps[:, 1, c * P:(c + 1) * P], W1T[:, c * P:(c + 1) * P], W2s[:, :],
                                    start=True, stop=True)
                last.then_inc(w12_done, 1)

            def turn_h(tiles):
                for t in tiles:
                    r, b = rows(t), t % 2
                    pe.wait_ge(h_ready, t + 1)
                    if t >= 2:
                        pe.wait_ge(hT_ready, t - 1)
                    for c in range(DC):
                        last = turn(ps[:, 6 + b, c * P:c * P + r], h[0:r, t, c * P:(c + 1) * P], r)
                    last.then_inc(h_turned, 1)

            def turn_h2(tiles):
                for t in tiles:
                    r, b = rows(t), t % 2
                    pe.wait_ge(h2_ready, t + 1)
                    if t >= 2:
                        pe.wait_ge(h2T_ready, t - 1)
                    for c in range(DC):
                        last = turn(ps[:, 3 + b, c * P:c * P + r], h2[0:r, b, c * P:(c + 1) * P], r)
                    last.then_inc(h2_turned, 1)

            def hh(group):
                pe.wait_ge(h2T_ready, (FIRST, REST)[group][-1] + 1)
                first = len(HH[0]) * group
                for i, (m, b) in enumerate(HH[group], start=first):
                    if i >= 3:
                        pe.wait_ge(hhT_ready, 1 + HH_BANKS[0:i].index(HH_BANKS[i]) if i == 3 else len(HH[0]))
                    for c in range(DC):
                        last = T.matmul(ps[:, HH_BANKS[i], 0:bank_len(b)], EW[:, c, m * P:(m + 1) * P],
                                        h2T[:, c, bank_of(b)], start=(c == 0), stop=(c == DC - 1))
                    last.then_inc(hh_done, 1)

            def sup(tiles):
                for t in tiles:
                    r = rows(t)
                    if t - 2 >= tiles[0]:
                        pe.wait_ge(sup_ready, t - 1)
                    for c in range(DC):
                        last = T.matmul(ps[0:r, sup_bank(t), 0:D + 1], h2T[:, c, nodes(t)], WN[:, c, :],
                                        start=(c == 0), stop=(c == DC - 1))
                    last.then_inc(sup_done, 1)

            def project(b, base, W, XT, XT_ready, done):
                pe.wait_ge(XT_ready, min(NT, (b + 1) * TB))
                for c in range(DC):
                    last = T.matmul(ps[:, base + b, 0:bank_len(b)], W[:, c, :], XT[:, c, bank_of(b)],
                                    start=(c == 0), stop=(c == DC - 1))
                last.then_inc(done, 1)

            def logits(s):
                pe.wait_ge(q2_copied, NB * (s + 1))
                pe.wait_ge(k_copied, s + 1)
                for t in range(NT):
                    r = rows(t)
                    if t >= 2:
                        pe.wait_ge(exp_done, s * NT + t - 1)
                    for b in range(NB):
                        last = T.matmul(ps[0:r, 3 * (t % 2) + b, 0:bank_len(b)], Q2T[:, nodes(t)], KT[:, bank_of(b)],
                                        start=True, stop=True)
                    last.then_inc(logits_done, 1)

            def sx():
                pe.wait_ge(st_diag, NT)
                for t in range(NT):
                    r = rows(t)
                    if t == 2:
                        pe.wait_ge(exp_done, NT)
                    if t >= 8:
                        pe.wait_ge(sx_ready, t - 7)
                    for k in range(NT):
                        q = rows(k)
                        last = T.matmul(ps[0:r, bank_at(t), 0:D + 1], ST[0:q, k, nodes(t)], reg_h[0:q, k, :],
                                        start=(k == 0), stop=(k == NT - 1))
                    last.then_inc(sx_done, 1)

            def turn_g(t):
                r, b = rows(t), t % 2
                if t >= 2:
                    pe.wait_ge(gT_ready, t - 1)
                for c in range(DC):
                    last = turn(ps[:, 4 + b, c * P:c * P + r], FB[0:r, t, c * P:(c + 1) * P], r)
                last.then_inc(g_turned, 1)

            def gu(t):
                r, b = rows(t), t % 2
                pe.wait_ge(gT_ready, t + 1)
                if t >= 2:
                    pe.wait_ge(gu_ready, t - 1)
                for d in range(2):
                    for c in range(DC):
                        last = T.matmul(ps[0:r, 2 * b + d, :], GT[:, b, c * P:c * P + r],
                                        U12[:, d, c, :, :].rearrange("p s n -> p (s n)"),
                                        start=(c == 0), stop=(c == DC - 1))
                last.then_inc(gu_done, 1)

            def x3():
                for t in range(NT):
                    r = rows(t)
                    if t == 2:
                        pe.wait_ge(exp_done, 2 * NT)
                    if t >= 8:
                        pe.wait_ge(x3_ready, t - 7)
                    for c in range(DC):
                        last = T.matmul(ps[0:r, bank_at(t), :], XaT[:, c, nodes(t)],
                                        U3s[:, c, :, :].rearrange("p s n -> p (s n)"),
                                        start=(c == 0), stop=(c == DC - 1))
                    last.then_inc(x3_done, 1)

            def sv(t):
                r = rows(t)
                pe.wait_ge(x3_ready, min(NT, t + NT - 7))
                if t >= 8:
                    pe.wait_ge(sv_ready, t - 7)
                for k in range(NT):
                    q = rows(k)
                    last = T.matmul(ps[0:r, bank_at(NT + t), :], ST[0:q, k, nodes(t)], FB[0:q, k, :],
                                    start=(k == 0), stop=(k == NT - 1))
                last.then_inc(sv_done, 1)

            def turn_blocks(base, src, r, done):
                for j in range(NT):
                    last = turn(ps[0:rows(j), base + j // TB, (j % TB) * P:(j % TB) * P + r], src[:, nodes(j)], r)
                    if j % TB == TB - 1 or j == NT - 1:
                        last.then_inc(done, 1)

            def weigh(t, n, rhs, width, ready, done):
                r, b = rows(t), t % 2
                for j in range(NT):
                    q = rows(j)
                    if j % TB == 0:
                        pe.wait_ge(ready, NB * n + j // TB + 1)
                    last = T.matmul(ps[0:r, 6 + b, 0:width], AT[0:q, b, j, 0:r], rhs[0:q, j, 0:width],
                                    start=(j == 0), stop=(j == NT - 1))
                last.then_inc(done, 1)

            def turn_xa(t):
                r, b = rows(t), t % 2
                pe.wait_ge(xa_ready, t + 1)
                for c in range(DC):
                    last = turn(ps[:, 6 + b, D + c * P:D + c * P + r], xa[0:r, b, c * P:(c + 1) * P], r)
                last.then_inc(xa_turned, 1)

            def attend(s):
                for t in range(NT):
                    g = s * NT + t
                    pe.wait_ge(A_ready, g + 1)
                    if t >= 1:
                        pe.wait_ge(AT_ready, NB * g)
                    turn_blocks(0, E[0:rows(t), t, :], rows(t), A_turned)
                    if s == 0 and t >= 1:
                        turn_xa(t - 1)
                    if t >= 2:
                        if s == 0:
                            pe.wait_ge(xaT_ready, t - 1)
                        else:
                            pe.wait_ge(y_ready, t - 1)
                    weigh(t, g, reg_h, D + s, AT_ready, ax_done)
                    if s == 0 and t > TB and t % TB == 1:
                        project(t // TB - 1, NB, W3s, XaT, xaT_ready, k_done)
                    if s == 1 and t == NT - 2:
                        pe.wait_ge(sp_in, 16 * 8)
                        turn_h2(FIRST)
                        hh(0)
                if s == 0:
                    turn_xa(NT - 1)

            def turn_needs(s):
                pe.wait_ge(need_ready, s + 1)
                turn(ps[0:NT, 6 if s == 0 else 1, 0:P], need[:, :], P).then_inc(need_turned, 1)

            pe.wait_ge(const_ready, 3)
            pe.wait_ge(w_in, 16 * 3)
            weights()
            for b in range(NB + 1):
                if b < NB:
                    turn_h(range(b * TB, min(NT, (b + 1) * TB)))
                if b >= 1:
                    project(b - 1, NB, W3s, hT, hT_ready, k_done)
                    if b == 1:
                        pe.wait_ge(w12_ready, 1)
                    project(b - 1, 0, W1s, hT, hT_ready, q2_done)
            logits(0)
            sx()
            pe.wait_ge(u_in, 16 * 6)
            pe.wait_ge(sx_ready, NT)
            turn_g(0)
            for t in range(NT):
                if t + 1 < NT:
                    turn_g(t + 1)
                gu(t)
                if t == HALVINGS[0] * SHARED - GU_SLOT:
                    turn_needs(0)
            pe.wait_ge(gu_ready, NT)
            attend(0)
            project(NB - 1, NB, W3s, XaT, xaT_ready, k_done)
            for b in range(NB):
                project(b, 0, W1s, XaT, xaT_ready, q2_done)
            logits(1)
            x3()
            for t in range(NT):
                sv(t)
            pe.wait_ge(sv_ready, NT)
            turn_needs(1)
            attend(1)

            pe.wait_ge(AT_ready, 2 * NB * NT)
            sup(FIRST)
            def edges(t, banks=range(NB)):
                r = rows(t)
                if t >= 1:
                    pe.wait_ge(em_ready, t)
                for b in banks:
                    for c in range(DC):
                        last = T.matmul(ps[0:r, b, 0:bank_len(b)], hhT[:, c, nodes(t)], hhT[:, c, bank_of(b)],
                                        start=(c == 0), stop=(c == DC - 1))
                if banks[-1] == NB - 1:
                    last.then_inc(e_done, 1)

            pe.wait_ge(hhT_ready, len(HH[0]))
            pe.wait_ge(sup_ready, len(FIRST))
            edges(0, range(NB - 1))
            turn_h2(REST)
            hh(1)

            pe.wait_ge(hhT_ready, len(HH[0]) + len(HH[1]))
            edges(0, range(NB - 1, NB))
            pe.wait_ge(y_ready, NT)
            sup(REST)
            edges(1)
            pe.wait_ge(sup_ready, NT)
            pe.wait_ge(score_max, 1)
            turn(ps[0:1, 7, 0:P], nmx[:, :], P).then_inc(score_turned, 1)
            pe.wait_ge(score_top, 1)
            T.matmul(ps[:, 7, 0:1], ones_row, nall[0:1, :], start=True, stop=True).then_inc(score_spread, 1)
            pe.wait_ge(score_sum, 1)
            T.matmul(ps[:, 7, 0:1], ones_all[:, :], ncol[:, :], start=True, stop=True).then_inc(score_tot, 1)
            for t in range(NT + 1):
                if 1 <= t < NT - 1:
                    edges(t + 1)
                if t < NT:
                    pe.wait_ge(pa_ready, t + 1)
                    if t >= 1:
                        pe.wait_ge(paT_ready, NB * t)
                    turn_blocks(3, em[0:rows(t), t % 2, :], rows(t), pa_turned)
                if t >= 1:
                    u = t - 1
                    if u == 1:
                        pe.wait_ge(natt_ready, 1)
                    if u >= 2:
                        pe.wait_ge(out_ready, u - 1)
                    weigh(u, u, support, D, paT_ready, out_sum)


_INS = ['x', 'adj', 'adj_t', 'L0_gnn_W1', 'L0_gnn_W2', 'L0_gnn_W3', 'L0_gnn_U1', 'L0_gnn_U2', 'L0_gnn_U3',
        'L0_gnn_gamma', 'L0_gnn_beta', 'L1_gnn_weight', 'L1_gnn_bias', 'L1_gnn_node_w', 'L1_gnn_edge_w']


def kernel(**inputs):
    import numpy as _np
    import concourse.bacc as _bacc
    from concourse import mybir as _mybir
    from concourse.bass_utils import run_bass_kernel_spmd as _run

    nc = _bacc.Bacc("TRN2", target_bir_lowering=False, num_devices=1)
    laid_out = dict(inputs, adj_t=_np.asarray(inputs['adj']).T)
    arrays, args = {}, []
    for name in _INS:
        a = _np.ascontiguousarray(laid_out[name])
        arrays[f"in_{name}_dram"] = a
        args.append(nc.dram_tensor(f"in_{name}_dram", a.shape, _mybir.dt.from_np(a.dtype), kind="ExternalInput").ap())
    y = nc.dram_tensor("out_0_dram", inputs['x'].shape, _mybir.dt.float32, kind="ExternalOutput").ap()
    gnn_block(nc, *args, y)
    r = _run(nc, [arrays], core_ids=[0])
    return r.results[0]["out_0_dram"]
```
